# Optimizing a Trainium2 kernel written in Bass

```python
import numpy as np
import jax
import jax.numpy as jnp

def _softmax(x, axis=-1):
    return jax.nn.softmax(x, axis=axis)

def _gelu(x):
    return jax.nn.gelu(x, approximate=True)

def _silu(x):
    return jax.nn.silu(x)

def _sigmoid(x):
    return jax.nn.sigmoid(x)

def _layernorm(x, axis=-1, eps=1e-05):
    m = jnp.mean(x, axis=axis, keepdims=True)
    v = jnp.var(x, axis=axis, keepdims=True)
    return (x - m) / jnp.sqrt(v + eps)

def _scatter_add(tgt, idx, src, axis=0):
    return tgt.at[idx].add(src)

def _segment_sum(src, seg, n):
    return jax.ops.segment_sum(src, seg, n)
kernel_name = 'mk_adaln_d1_jaxref_r4_4b7ff3'

def setup_inputs(seed: int=0):
    np.random.seed(seed)
    _w = jnp.asarray

    def _L0_attn_setup():
        import jax, jax.numpy as jnp
        import numpy as np
        B, S, D = (4, 512, 256)
        key = jax.random.key(seed)
        kx, kq, kk, kv = jax.random.split(key, 4)
        bound = float(np.sqrt(6.0 / (D + D)))
        return {'x': jax.random.normal(kx, (B, S, D), dtype=jnp.float32), 'WQ': jax.random.uniform(kq, (D, D), jnp.float32, -bound, bound), 'WK': jax.random.uniform(kk, (D, D), jnp.float32, -bound, bound), 'WV': jax.random.uniform(kv, (D, D), jnp.float32, -bound, bound)}
    _L0_attn_in = _L0_attn_setup()

    def _L0_ffn_setup():
        import jax, jax.numpy as jnp
        import numpy as np
        D_MODEL = 256
        M = 64
        INNER = 16
        key = jax.random.key(seed)
        ks = jax.random.split(key, 9)

        def init(k, shape, fan_in):
            bound = 1.0 / np.sqrt(fan_in)
            return jax.random.uniform(k, shape, jnp.float32, -bound, bound)
        x = jax.random.normal(ks[0], (16, 1024, D_MODEL), dtype=jnp.float32)
        Win = init(ks[1], (D_MODEL, M), D_MODEL)
        bin_ = init(ks[2], (M,), D_MODEL)
        W1 = init(ks[3], (M, INNER), 1)
        b1 = init(ks[4], (M, INNER), 1)
        W2 = init(ks[5], (M, INNER), INNER)
        b2 = init(ks[6], (M,), INNER)
        Wout = init(ks[7], (M, D_MODEL), M)
        bout = init(ks[8], (D_MODEL,), M)
        return {'x': x, 'Win': Win, 'bin_': bin_, 'W1': W1, 'b1': b1, 'W2': W2, 'b2': b2, 'Wout': Wout, 'bout': bout}
    _L0_ffn_in = _L0_ffn_setup()
    _L0_c = _w((lambda *s: np.random.randn(*s).astype(np.float32) * 0.05)(8, 256))
    _L0_wmod = _w((lambda *s: np.random.randn(*s).astype(np.float32) * 0.05)(256, 6 * 256) * 256 ** (-0.5))
    _d = {'L0_attn_x': _L0_attn_in['x'], 'L0_attn_WQ': _L0_attn_in['WQ'], 'L0_attn_WK': _L0_attn_in['WK'], 'L0_attn_WV': _L0_attn_in['WV'], 'L0_ffn_Win': _L0_ffn_in['Win'], 'L0_ffn_bin_': _L0_ffn_in['bin_'], 'L0_ffn_W1': _L0_ffn_in['W1'], 'L0_ffn_b1': _L0_ffn_in['b1'], 'L0_ffn_W2': _L0_ffn_in['W2'], 'L0_ffn_b2': _L0_ffn_in['b2'], 'L0_ffn_Wout': _L0_ffn_in['Wout'], 'L0_ffn_bout': _L0_ffn_in['bout'], 'L0_c': _L0_c, 'L0_wmod': _L0_wmod}
    _x0 = _d['L0_attn_x']
    _d['L0_attn_x'] = jax.random.normal(jax.random.fold_in(jax.random.key(seed), 1), (8, 512, 256), dtype=_x0.dtype)
    del _x0
    return _d

def reference(L0_attn_x, L0_attn_WQ, L0_attn_WK, L0_attn_WV, L0_ffn_Win, L0_ffn_bin_, L0_ffn_W1, L0_ffn_b1, L0_ffn_W2, L0_ffn_b2, L0_ffn_Wout, L0_ffn_bout, L0_c, L0_wmod):

    def _L0_attn_ref(x, WQ, WK, WV):
        import jax, jax.numpy as jnp
        import numpy as np
        B, S, D = (4, 512, 256)
        dk = WQ.shape[1]
        q = x @ WQ
        k = x @ WK
        v = x @ WV
        scores = jnp.einsum('bsd,btd->bst', q, k) / jnp.sqrt(jnp.asarray(dk, x.dtype))
        s = x.shape[1]
        causal = jnp.tril(jnp.ones((s, s), dtype=bool))
        scores = jnp.where(causal[None, :, :], scores, jnp.asarray(-jnp.inf, x.dtype))
        attention = jax.nn.softmax(scores, axis=-1)
        return jnp.einsum('bst,btd->bsd', attention, v)

    def _L0_ffn_ref(x, Win, bin_, W1, b1, W2, b2, Wout, bout):
        import jax, jax.numpy as jnp
        import numpy as np
        D_MODEL = 256
        M = 64
        INNER = 16
        s = jnp.einsum('btd,dm->btm', x, Win) + bin_
        h = jax.nn.relu(s[..., None] * W1 + b1)
        g = jnp.einsum('btmh,mh->btm', h, W2) + b2
        out = jnp.einsum('btm,md->btd', g, Wout) + bout
        return out
    x = L0_attn_x
    mod = (_silu(L0_c) @ L0_wmod).reshape(L0_c.shape[0], 6, 1, -1)
    sa, ca, ga, sb, cb, gb = (mod[:, 0], mod[:, 1], mod[:, 2], mod[:, 3], mod[:, 4], mod[:, 5])
    ga = (2 * (ga >= 0) - 1) * jnp.maximum(jnp.abs(ga), 0.25)
    gb = (2 * (gb >= 0) - 1) * jnp.maximum(jnp.abs(gb), 0.25)
    h = _layernorm(x, axis=-1) * (1 + ca) + sa
    x = x + ga * _L0_attn_ref(h, L0_attn_WQ, L0_attn_WK, L0_attn_WV)
    h = _layernorm(x, axis=-1) * (1 + cb) + sb
    x = x + gb * _L0_ffn_ref(h, L0_ffn_Win, L0_ffn_bin_, L0_ffn_W1, L0_ffn_b1, L0_ffn_W2, L0_ffn_b2, L0_ffn_Wout, L0_ffn_bout)
    return x

_drawn_inputs = setup_inputs


def setup_inputs(seed=0):
    import zlib

    import numpy as np

    out = dict(_drawn_inputs(seed))
    spreads = {}
    factors = {'L0_ffn_Win': 3.397, 'L0_ffn_bin_': 8.0, 'L0_ffn_W1': 3.351, 'L0_ffn_bout': 3.224}
    for name, (base, spread) in spreads.items():
        noise = np.random.default_rng([zlib.crc32(name.encode()), seed]).standard_normal(out[name].shape)
        drawn = base * np.exp(spread * noise) if base else spread * noise
        out[name] = jnp.asarray(drawn.astype(out[name].dtype))
    for name, factor in factors.items():
        out[name] = (out[name] * factor).astype(out[name].dtype)
    return out
```

```python
import concourse.bass as bass
from concourse import mybir
from contextlib import ExitStack


def adaln_layer(nc, x, WQ, WK, WV, Win, bin_, W1, b1, W2, b2, Wout, bout, c, wmod, out):
    fp32, fp32r, bf16 = mybir.dt.float32, mybir.dt.float32r, mybir.dt.bfloat16
    ALU, ACT, AX = mybir.AluOpType, mybir.ActivationFunctionType, mybir.AxisListType

    B, S, D = x.shape
    P = 128
    NT = S // P
    KD = D // P
    M, INNER = W1.shape
    NJ = INNER // 2
    HALF = NT // 2
    SCALE = float(D) ** -0.5
    EPS = 1e-5
    GATE_MIN = 0.25
    MASKED = -1.0e38
    SA, CA, GA, SB, CB, GB = range(6)
    MIN_N = 256
    RING = 4

    ctx = ExitStack()
    with ctx:
        def sb(name, shape, dt=fp32):
            return ctx.enter_context(nc.sbuf_tensor(name, shape, dt))

        def sem(name):
            return ctx.enter_context(nc.semaphore(name))

        def f(ap):
            return ap.bitcast(fp32)

        ident = sb("ident", [P, P])
        ident_bf = sb("ident_bf", [P, P], bf16)
        mask_bf = sb("mask_bf", [P, P], bf16)
        minus_half = sb("minus_half", [P, NT])
        ones2 = sb("ones2", [2, P], fp32r)
        wq = sb("wq", [P, KD, D])
        wk = sb("wk", [P, KD, D])
        wqT = sb("wqT", [P, KD, D])
        wkT = sb("wkT", [P, KD, D])
        m_hi = sb("m_hi", [P, KD, D], fp32r)
        m_lo = sb("m_lo", [P, KD, D], fp32r)
        wv = sb("wv", [P, KD, D])
        wv_hi = sb("wv_hi", [P, KD, D], fp32r)
        wv_lo = sb("wv_lo", [P, KD, D], fp32r)
        win = sb("win", [P, KD, 2, M])
        win_hi = sb("win_hi", [P, KD, 2 * M], fp32r)
        win_lo = sb("win_lo", [P, KD, 2 * M], fp32r)
        wout = sb("wout", [P, D])
        w1c = sb("w1c", [P, NJ])
        b1c = sb("b1c", [P, NJ])
        w2c = sb("w2c", [P, NJ])
        b2c = sb("b2c", [P, 1])
        binc = sb("binc", [P, 1])
        relu_bias = sb("relu_bias", [P, NJ])
        c_sb = sb("c_sb", [B, D])
        c_exp = sb("c_exp", [B, D])
        c_den = sb("c_den", [B, D])
        c_sig = sb("c_sig", [B, D])
        c_silu = sb("c_silu", [B, D])
        siluT = sb("siluT", [P, KD, B])
        wmod_sb = sb("wmod_sb", [P, KD, 6, D])
        mod = sb("mod", [P, 4, KD, B])
        gate_sign = sb("gate_sign", [B, 2, D])
        gate_abs = sb("gate_abs", [B, 2, D])
        gate_neg = sb("gate_neg", [B, 2, D])
        gate = sb("gate", [B, 2, D])
        bout_sb = sb("bout_sb", [B, D])
        boutg = sb("boutg", [B, D])
        boutg_hi = sb("boutg_hi", [B, D], fp32r)
        boutg_lo = sb("boutg_lo", [B, D], fp32r)
        gates = sb("gates", [P, B, 2, D])
        bout2 = sb("bout2", [2, B, D], fp32r)
        xs = sb("xs", [P, B, NT, D])
        stat = [sb(f"stat{n}", [P, NT, 6]) for n in (1, 2)]
        mv = [sb(f"mv{n}", [P, NT, 2]) for n in (1, 2)]
        veps = [sb(f"veps{n}", [P, NT]) for n in (1, 2)]
        rstd = [sb(f"rstd{n}", [P, NT]) for n in (1, 2)]
        nmr = [sb(f"nmr{n}", [P, NT]) for n in (1, 2)]
        xn = [sb(f"xn{n}", [P, NT, D]) for n in (1, 2)]
        h_full = [sb(f"h_full{n}", [P, KD, S]) for n in (1, 2)]
        h_hi = [sb(f"h_hi{n}", [P, KD, S], fp32r) for n in (1, 2)]
        h_lo = [sb(f"h_lo{n}", [P, KD, S], fp32r) for n in (1, 2)]
        t_hi = sb("t_hi", [P, KD, S], fp32r)
        t_lo = sb("t_lo", [P, KD, S], fp32r)
        v_hi = sb("v_hi", [P, NT, D], fp32r)
        v_lo = sb("v_lo", [P, NT, D], fp32r)
        negmax = sb("negmax", [P, NT])
        den = sb("den", [P, NT])
        rden = sb("rden", [P, NT])
        probs = [sb(f"probs{i}", [P, (i + 1) * P]) for i in range(NT)]
        GROUPS = [[0, 1], [2], [3]]
        pt_hi = [sb(f"pt_hi{g}", [P, sum(i + 1 for i in q), P], fp32r) for g, q in enumerate(GROUPS)]
        pt_lo = [sb(f"pt_lo{g}", [P, sum(i + 1 for i in q), P], fp32r) for g, q in enumerate(GROUPS)]
        NG = len(GROUPS)
        y = sb("y", [P, NT, D])
        relu = [sb(f"relu{k}", [P, S]) for k in range(RING)]
        acc = sb("acc", [P, S])
        g_hi = sb("g_hi", [P, S], fp32r)
        g_lo = sb("g_lo", [P, S], fp32r)
        wog = sb("wog", [P, D])
        wog_hi = sb("wog_hi", [P, D], fp32r)
        wog_lo = sb("wog_lo", [P, D], fp32r)

        def pt_slot(i, j):
            g = next(n for n, q in enumerate(GROUPS) if i in q)
            return g, sum(k + 1 for k in GROUPS[g] if k < i) + j

        def bank(name):
            return ctx.enter_context(nc.psum_tensor(name, [P, S], fp32))

        A = [bank("A0"), bank("A1")]
        SC = [bank("B0"), bank("B1")]
        C = [bank("C0"), bank("C1")]
        E = [bank("D0"), bank("D1")]

        gate_dram = nc.dram_tensor("gate_scratch", [B, 2 * D], fp32)
        bout_dram = nc.dram_tensor("bout_scratch", [2, B, D], fp32)

        c_in, wmod_in, wmod2_in = sem("c_in"), sem("wmod_in"), sem("wmod2_in")
        wqk_in, wv_in, win_in, small_in, bout_in = sem("wqk_in"), sem("wv_in"), sem("win_in"), sem("small_in"), sem("bout_in")
        consts, b2_zero = sem("consts"), sem("b2_zero")
        c_exped, c_steps, siluT_pe, siluT_sb = sem("c_exped"), sem("c_steps"), sem("siluT_pe"), sem("siluT_sb")
        wT_pe, wT_sb, m_pe, m_hi_sb, m_lo_sb = sem("wT_pe"), sem("wT_sb"), sem("m_pe"), sem("m_hi_sb"), sem("m_lo_sb")
        w_hi_sb, w_lo_sb = sem("w_hi_sb"), sem("w_lo_sb")
        mod_pe, mod_sb, gate_pe, gate_steps = sem("mod_pe"), sem("mod_sb"), sem("gate_pe"), sem("gate_steps")
        gate_out, bout_out, gates_in, bout2_in = sem("gate_out"), sem("bout_out"), sem("gates_in"), sem("bout2_in")
        rbias = sem("rbias")
        x_in = sem("x_in")
        stat_d = [sem(f"stat_d{n}") for n in (1, 2)]
        aggr_d = [sem(f"aggr_d{n}") for n in (1, 2)]
        veps_d = [sem(f"veps_d{n}") for n in (1, 2)]
        rstd_p = [sem(f"rstd_p{n}") for n in (1, 2)]
        nmr_d = [sem(f"nmr_d{n}") for n in (1, 2)]
        xn_p = [sem(f"xn_p{n}") for n in (1, 2)]
        xT_pe = [sem(f"xT_pe{n}") for n in (1, 2)]
        h_full_a = [sem(f"h_full_a{n}") for n in (1, 2)]
        h_hi_d = [sem(f"h_hi_d{n}") for n in (1, 2)]
        h_lo_d = [sem(f"h_lo_d{n}") for n in (1, 2)]
        t_pe, t_hi_a, t_lo_d = sem("t_pe"), sem("t_hi_a"), sem("t_lo_d")
        v_pe, v_hi_a, v_lo_d = sem("v_pe"), sem("v_hi_a"), sem("v_lo_d")
        sc_pe, max_d, exp_a = sem("sc_pe"), sem("max_d"), sem("exp_a")
        pt_pe, pt_hi_a, pt_lo_d = sem("pt_pe"), sem("pt_hi_a"), sem("pt_lo_d")
        rden_d, pv_pe, y_d, x2_p = sem("rden_d"), sem("pv_pe"), sem("y_d"), sem("x2_p")
        s_pe, relu_a, acc_d = sem("s_pe"), sem("relu_a"), sem("acc_d")
        g_hi_d, g_lo_d = sem("g_hi_d"), sem("g_lo_d")
        wog_p, wog_hi_a, wog_lo_p = sem("wog_p"), sem("wog_hi_a"), sem("wog_lo_p")
        o_pe, fin_d, stored = sem("o_pe"), sem("fin_d"), sem("stored")

        block = ctx.enter_context(nc.Block())

        LAST_LAG = 3

        def steps(step):
            for i in range(-1, B + LAST_LAG):
                step(i, lambda b: 0 <= b < B)

        @block.sync
        def _(sp):
            x_v = x.rearrange("b (i p) d -> p b i d", p=P)
            out_v = out.rearrange("b (i p) d -> p b i d", p=P)

            def load(b):
                sp.dma_start(xs[:, b, :, :], x_v[:, b, :, :]).then_inc(x_in, 16)

            def store(b, h):
                sp.wait_ge(fin_d, 2 * b + h + 1)
                sp.dma_start(out_v[:, b, HALF * h:HALF * (h + 1), :],
                             xs[:, b, HALF * h:HALF * (h + 1), :]).then_inc(stored, 16)

            load(0)
            sp.dma_start(wq[:, :, :], WQ.rearrange("(k p) e -> p k e", p=P)).then_inc(wqk_in, 16)
            sp.dma_start(wk[:, :, :], WK.rearrange("(k p) e -> p k e", p=P)).then_inc(wqk_in, 16)
            sp.dma_start(wv[:, :, :], WV.rearrange("(k p) e -> p k e", p=P)).then_inc(wv_in, 16)
            for r in range(2):
                sp.dma_start(win[:, :, r, :], Win.rearrange("(k p) m -> p k m", p=P)).then_inc(win_in, 16)
            sp.wait_ge(b2_zero, 1)
            for r in range(2):
                q = slice(r * M, (r + 1) * M)
                sp.dma_start(w1c[q, :], W1[:, r * NJ:(r + 1) * NJ]).then_inc(small_in, 16)
                sp.dma_start(b1c[q, :], b1[:, r * NJ:(r + 1) * NJ]).then_inc(small_in, 16)
                sp.dma_start(w2c[q, :], W2[:, r * NJ:(r + 1) * NJ]).then_inc(small_in, 16)
                sp.dma_start(binc[q, :], bin_.rearrange("(m a) -> m a", a=1)).then_inc(small_in, 16)
                sp.dma_start(wout[q, :], Wout[:, :]).then_inc(small_in, 16)
            sp.dma_start(b2c[0:M, :], b2.rearrange("(m a) -> m a", a=1)).then_inc(small_in, 16)
            sp.wait_ge(x_in, 16)
            load(1)
            sp.wait_ge(gate_steps, 5)
            sp.dma_start(gate_dram[:, :], gate[:, :, :].rearrange("b n d -> b (n d)")).then_inc(gate_out, 16)
            sp.wait_ge(gate_out, 16)
            sp.dma_start(gates[:, :, :, :].rearrange("p b n d -> p (b n d)"),
                         gate_dram[:, :].rearrange("b n -> (b n)").partition_broadcast(P)).then_inc(gates_in, 16)
            sp.wait_ge(gate_steps, 8)
            sp.dma_start(bout_dram[0, :, :], f(boutg_hi[:, :])).then_inc(bout_out, 16)
            sp.dma_start(bout_dram[1, :, :], f(boutg_lo[:, :])).then_inc(bout_out, 16)
            sp.wait_ge(bout_out, 32)
            sp.dma_start(f(bout2[:, :, :]), bout_dram[:, :, :]).then_inc(bout2_in, 16)

            def step(i, live):
                if live(i + 2):
                    sp.wait_ge(x_in, 16 * (i + 2))
                    load(i + 2)
                if live(i - 3):
                    store(i - 3, 0)
                    store(i - 3, 1)

            steps(lambda i, live: step(i, live) if i >= 0 else None)
            sp.wait_ge(stored, 2 * B * 16)

        @block.gpsimd
        def _(pool):
            pool.memset(b2c[:, :], 0.0).then_inc(b2_zero, 1)
            pool.memset(ident[:, :], 0.0).then_inc(consts, 1)
            pool.memset(mask_bf[:, :], 0.0).then_inc(consts, 1)
            pool.memset(minus_half[:, :], -0.5).then_inc(consts, 1)
            pool.memset(f(ones2[:, :]), 1.0).then_inc(consts, 1)
            pool.memset(ident_bf[:, :], 0.0).then_inc(consts, 1)
            pool.wait_ge(consts, 5)
            for m in (ident, ident_bf):
                pool.affine_select(out=m[:, :], in_=m[:, :], compare_op=ALU.not_equal, fill=1.0, base=0,
                                   pattern=[[-1, P]], channel_multiplier=1).then_inc(consts, 1)
            pool.affine_select(out=mask_bf[:, :], in_=mask_bf[:, :], compare_op=ALU.is_ge, fill=MASKED, base=0,
                               pattern=[[-1, P]], channel_multiplier=1).then_inc(consts, 1)

            def rsqrt(n, b):
                pool.wait_ge(veps_d[n], b + 1)
                if first(b):
                    pool.wait_ge(xn_p[n], NT * b)
                    pool.wait_ge(nmr_d[n], b)
                pool.tensor_tensor(rstd[n][:, :], veps[n][:, :], minus_half[:, :], ALU.pow).then_inc(rstd_p[n], 1)

            def normalise(n, b):
                pool.wait_ge(nmr_d[n], b + 1)
                if first(b):
                    pool.wait_ge(xT_pe[n], KD * b)
                for i in range(NT):
                    pool.tensor_scalar(xn[n][:, i, :], xs[:, b, i, :], rstd[n][:, i:i + 1], nmr[n][:, i:i + 1],
                                       ALU.mult, ALU.add).then_inc(xn_p[n], 1)

            def first(b):
                return not (isinstance(b, int) and b == 0)

            def gate_wout(b):
                if not first(b):
                    pool.wait_ge(small_in, 11 * 16)
                    pool.wait_ge(gates_in, 16)
                if first(b):
                    pool.wait_ge(o_pe, 2 * b)
                    pool.wait_ge(wog_lo_p, b)
                pool.tensor_tensor(wog[:, :], wout[:, :], gates[:, b, 1, :], ALU.mult).then_inc(wog_p, 1)
                pool.wait_ge(wog_hi_a, b + 1)
                pool.tensor_tensor(wog_lo[:, :], wog[:, :], f(wog_hi[:, :]), ALU.subtract).then_inc(wog_lo_p, 1)

            def add_attention(b, h):
                pool.wait_ge(y_d, NT * b + HALF * (h + 1))
                q = slice(HALF * h, HALF * (h + 1))
                pool.tensor_tensor(xs[:, b, q, :], xs[:, b, q, :], y[:, q, :], ALU.add).then_inc(x2_p, 1)

            def step(i, live):
                if live(i - 2):
                    rsqrt(1, i - 2)
                    normalise(1, i - 2)
                    gate_wout(i - 2)
                if live(i + 1):
                    rsqrt(0, i + 1)
                    normalise(0, i + 1)
                if live(i - 1):
                    add_attention(i - 1, 0)
                    add_attention(i - 1, 1)

            steps(step)

        @block.scalar
        def _(act):
            act.dma_start(c_sb[:, :], c).then_inc(c_in, 16)
            wm = wmod.rearrange("(k p) (q d) -> p k q d", p=P, d=D)
            act.dma_start(wmod_sb[:, :, SA:CA + 1, :], wm[:, :, SA:CA + 1, :]).then_inc(wmod_in, 16)
            act.dma_start(wmod_sb[:, :, GA:GB + 1, :], wm[:, :, GA:GB + 1, :]).then_inc(wmod2_in, 16)
            act.dma_start(bout_sb[:, :], bout.partition_broadcast(B)).then_inc(bout_in, 16)
            act.wait_ge(c_in, 16)
            act.activation(c_exp[:, :], c_sb[:, :], ACT.Exp, scale=-1.0).then_inc(c_exped, 1)
            for n, dst in enumerate((wqT, wkT)):
                act.wait_ge(wT_pe, n + 1)
                act.activation(dst[:, :, :], SC[n][:, :].rearrange("p (k d) -> p k d", k=KD), ACT.Copy).then_inc(wT_sb, 1)
            act.wait_ge(m_pe, 1)
            act.activation(m_hi[:, :, :], C[0][:, :].rearrange("p (k d) -> p k d", k=KD), ACT.Copy,
                           scale=SCALE).then_inc(m_hi_sb, 1)

            def modulate(n, b):
                for k in range(KD):
                    act.wait_ge(xT_pe[n], KD * b + k + 1)
                    if n == 0 and first(b) is False and k == 0:
                        act.wait_ge(mod_sb, 1)
                    if n == 1 and first(b) is False and k == 0:
                        act.wait_ge(mod_sb, 2)
                    if first(b):
                        act.wait_ge(h_lo_d[n], KD * (b - 1) + k + 1)
                    act.activation(h_full[n][:, k, :], (A, E)[n][k][:, :], ACT.Identity,
                                   bias=mod[:, 2 * n, k, b:b + 1],
                                   scale=mod[:, 2 * n + 1, k, b:b + 1]).then_inc(h_full_a[n], 1)

            def first(b):
                return not (isinstance(b, int) and b == 0)

            def exps(b, i):
                act.wait_ge(max_d, NT * b + i + 1)
                if first(b):
                    act.wait_ge(pt_pe, NG * b)
                    act.wait_ge(rden_d, b)
                act.activation(probs[i][:, :], SC[i % 2][:, 0:(i + 1) * P], ACT.Exp, bias=negmax[:, i:i + 1],
                               accum_out=den[:, i:i + 1]).then_inc(exp_a, 1)

            def round_pt(b, g):
                n = pt_hi[g].shape[1]
                act.wait_ge(pt_pe, NG * b + g + 1)
                if first(b):
                    act.wait_ge(pv_pe, 2 * b)
                act.activation(pt_hi[g][:, :, :], C[g % 2][:, 0:n * P].rearrange("p (n q) -> p n q", q=P),
                               ACT.Copy).then_inc(pt_hi_a, 1)

            def round_t(b, m):
                act.wait_ge(t_pe, KD * b + m + 1)
                if first(b):
                    act.wait_ge(sc_pe, NT * b)
                act.activation(t_hi[:, m, :], A[m][:, :], ACT.Copy).then_inc(t_hi_a, 1)

            def round_v(b, h):
                act.wait_ge(v_pe, 2 * b + h + 1)
                if first(b):
                    act.wait_ge(pv_pe, 2 * b)
                act.activation(v_hi[:, HALF * h:HALF * (h + 1), :], A[h][:, :].rearrange("p (i d) -> p i d", d=D),
                               ACT.Copy).then_inc(v_hi_a, 1)

            def round_wog(b):
                act.wait_ge(wog_p, b + 1)
                if first(b):
                    act.wait_ge(o_pe, 2 * b)
                act.activation(wog_hi[:, :], wog[:, :], ACT.Copy).then_inc(wog_hi_a, 1)

            def relus(b, j):
                if j == 0:
                    act.wait_ge(s_pe, b + 1)
                    if not first(b):
                        act.wait_ge(rbias, 2)
                n = NJ * b + j
                if first(b) or j >= RING:
                    act.wait_ge(acc_d, n - RING + 1)
                act.activation(relu[j % RING][:, :], E[0][:, :], ACT.Relu, bias=relu_bias[:, j:j + 1],
                               scale=w1c[:, j:j + 1]).then_inc(relu_a, 1)

            def step(i, live):
                if live(i - 1):
                    for k in range(NT):
                        exps(i - 1, k)
                if live(i):
                    modulate(0, i)
                if live(i - 2):
                    modulate(1, i - 2)
                    round_wog(i - 2)
                if live(i - 1):
                    for g in range(NG):
                        round_pt(i - 1, g)
                if live(i):
                    for m in range(KD):
                        round_t(i, m)
                if live(i - 2):
                    for j in range(NJ - 2):
                        relus(i - 2, j)
                if live(i):
                    round_v(i, 0)
                if live(i - 2):
                    relus(i - 2, NJ - 2)
                    relus(i - 2, NJ - 1)
                if live(i):
                    round_v(i, 1)

            steps(step)

        @block.tensor
        def _(pe):
            def three(dst, lhs, rhs, parts, inc=None, open_=False):
                n = len(parts)
                for q, part in enumerate(parts):
                    lh, ll, rh, rl = lhs[0](part), lhs[1](part), rhs[0](part), rhs[1](part)
                    pe.matmul(dst, ll, rh, start=(q == 0), stop=False)
                    pe.matmul(dst, lh, rl, start=False, stop=False)
                    mm = pe.matmul(dst, lh, rh, start=False, stop=(q == n - 1 and not open_))
                return mm

            def first(b):
                return not (isinstance(b, int) and b == 0)

            pe.wait_ge(consts, 8)
            pe.wait_ge(wqk_in, 32)
            for n, w in enumerate((wq, wk)):
                for e in range(KD):
                    for d in range(KD):
                        mm = pe.transpose(SC[n][:, e * D + d * P:e * D + (d + 1) * P],
                                          w[:, d, e * P:(e + 1) * P], ident[:, :])
                mm.then_inc(wT_pe, 1)
            pe.wait_ge(c_steps, 3)
            for k in range(KD):
                mm = pe.transpose(E[0][:, k * B:(k + 1) * B], c_silu[:, k * P:(k + 1) * P], ident[0:B, 0:B])
            mm.then_inc(siluT_pe, 1)
            pe.wait_ge(wT_sb, 2)
            for d in range(KD):
                for e in range(KD):
                    mm = pe.matmul(C[0][:, d * D:(d + 1) * D], wqT[:, e, d * P:(d + 1) * P], wkT[:, e, :],
                                   start=(e == 0), stop=(e == KD - 1))
            mm.then_inc(m_pe, 1)
            pe.wait_ge(siluT_sb, 1)

            def modulation(n, qs):
                for q, which in enumerate(qs):
                    for k in range(KD):
                        for e in range(KD):
                            col = ((2 * n + q) * KD + k) * B
                            mm = pe.matmul(E[1][:, col:col + B], wmod_sb[:, e, which, k * P:(k + 1) * P],
                                           siluT[:, e, :], start=(e == 0), stop=(e == KD - 1))
                mm.then_inc(mod_pe, 1)

            def transpose_x(n, b):
                pe.wait_ge(xn_p[n], NT * (b + 1))
                if n == 0 and first(b):
                    pe.wait_ge(v_lo_d, 2 * b)
                if n == 1:
                    pe.wait_ge(mod_sb, 2)
                    if first(b):
                        pe.wait_ge(fin_d, 2 * b)
                for k in range(KD):
                    for i in range(NT):
                        mm = pe.transpose((A, E)[n][k][:, i * P:(i + 1) * P], xn[n][:, i, k * P:(k + 1) * P], ident[:, :])
                    mm.then_inc(xT_pe[n], 1)

            def project_t(b):
                if not first(b):
                    pe.wait_ge(m_lo_sb, 1)
                pe.wait_ge(h_lo_d[0], KD * (b + 1))
                for m in range(KD):
                    three(A[m][:, :],
                          [lambda k, w=w, m=m: w[:, k, m * P:(m + 1) * P] for w in (m_hi, m_lo)],
                          [lambda k, w=w: w[:, k, :] for w in (h_hi[0], h_lo[0])], range(KD)).then_inc(t_pe, 1)

            def project_v(b):
                if not first(b):
                    pe.wait_ge(w_lo_sb, 1)
                for h in range(2):
                    pe.wait_ge(t_lo_d, KD * b + h + 1)
                    for n in range(HALF):
                        i = HALF * h + n
                        mm = three(A[h][:, n * D:(n + 1) * D],
                                   [lambda k, w=w, i=i: w[:, k, i * P:(i + 1) * P] for w in (h_hi[0], h_lo[0])],
                                   [lambda k, w=w: w[:, k, :] for w in (wv_hi, wv_lo)], range(KD))
                    mm.then_inc(v_pe, 1)

            def scores(b, i):
                if i == 0:
                    pe.wait_ge(t_lo_d, KD * (b + 1))
                if first(b) or i >= 2:
                    pe.wait_ge(exp_a, NT * b + i - 1)
                width = max((i + 1) * P, MIN_N)
                dst = SC[i % 2]
                three(dst[:, 0:width],
                      [lambda k, w=w: w[:, k, i * P:(i + 1) * P] for w in (t_hi, t_lo)],
                      [lambda k, w=w: w[:, k, 0:width] for w in (h_hi[0], h_lo[0])], range(KD), open_=True)
                pe.matmul(dst[:, i * P:(i + 1) * P], ident_bf[:, :], mask_bf[:, :], start=False,
                          stop=True).then_inc(sc_pe, 1)

            def transpose_p(b, g):
                pe.wait_ge(exp_a, NT * b + GROUPS[g][-1] + 1)
                if g < 2:
                    if first(b):
                        pe.wait_ge(y_d, NT * b)
                else:
                    pe.wait_ge(pt_lo_d, NG * b + 1)
                for i in GROUPS[g]:
                    for j in range(i + 1):
                        s = pt_slot(i, j)[1]
                        mm = pe.transpose(C[g % 2][:, s * P:(s + 1) * P], probs[i][:, j * P:(j + 1) * P], ident[:, :])
                mm.then_inc(pt_pe, 1)

            def attend(b, h):
                pe.wait_ge(pt_lo_d, NG * b + 2 + h)
                pe.wait_ge(v_lo_d, 2 * b + 1 + h)
                for n in range(HALF):
                    i = HALF * h + n
                    g = pt_slot(i, 0)[0]
                    mm = three(C[1 - h][:, n * D:(n + 1) * D],
                               [lambda j, w=w: w[g][:, pt_slot(i, j)[1], :] for w in (pt_hi, pt_lo)],
                               [lambda j, w=w: w[:, j, :] for w in (v_hi, v_lo)], range(i + 1))
                mm.then_inc(pv_pe, 1)

            def hidden(b):
                if not first(b):
                    pe.wait_ge(w_lo_sb, 2)
                pe.wait_ge(h_lo_d[1], KD * (b + 1))
                three(E[0][:, :],
                      [lambda k, w=w: w[:, k, :] for w in (win_hi, win_lo)],
                      [lambda k, w=w: w[:, k, :] for w in (h_hi[1], h_lo[1])], range(KD)).then_inc(s_pe, 1)

            def output(b):
                pe.wait_ge(g_lo_d, b + 1)
                pe.wait_ge(wog_lo_p, b + 1)
                if not first(b):
                    pe.wait_ge(bout2_in, 16)
                for h in range(2):
                    for n in range(HALF):
                        i = HALF * h + n
                        dst = E[1 - h][:, n * D:(n + 1) * D]
                        three(dst,
                              [lambda _, w=w, i=i: w[:, i * P:(i + 1) * P] for w in (g_hi, g_lo)],
                              [lambda _, w=w: w[:, :] for w in (wog_hi, wog_lo)], range(1), open_=True)
                        mm = pe.matmul(dst, ones2[:, :], bout2[:, b, :], start=False, stop=True)
                    mm.then_inc(o_pe, 1)

            def set_up_rest():
                pe.wait_ge(wmod2_in, 16)
                pe.wait_ge(mod_sb, 1)
                modulation(1, (SB, CB))
                for n, which in enumerate((GA, GB)):
                    for e in range(KD):
                        mm = pe.matmul(C[1][0:B, n * D:(n + 1) * D], siluT[:, e, :], wmod_sb[:, e, which, :],
                                       start=(e == 0), stop=(e == KD - 1))
                mm.then_inc(gate_pe, 1)

            def step(i, live):
                if live(i - 1):
                    for k in range(NT):
                        scores(i - 1, k)
                if live(i) and i >= 0:
                    transpose_x(0, i)
                if live(i - 3):
                    output(i - 3)
                if live(i - 2):
                    transpose_x(1, i - 2)
                if live(i - 1):
                    for g in range(NG):
                        transpose_p(i - 1, g)
                if live(i):
                    project_t(i)
                if live(i - 2):
                    hidden(i - 2)
                if live(i - 1):
                    attend(i - 1, 0)
                    attend(i - 1, 1)
                if live(i):
                    project_v(i)

            pe.wait_ge(wmod_in, 16)
            modulation(0, (SA, CA))
            set_up_rest()
            steps(step)

        @block.vector
        def _(dve):
            def first(b):
                return not (isinstance(b, int) and b == 0)

            def statistics(n, b):
                for i in range(NT):
                    if n == 0:
                        if i == 0:
                            dve.wait_ge(x_in, 16 * (b + 1))
                    elif i % HALF == 0:
                        dve.wait_ge(x2_p, 2 * b + i // HALF + 1)
                    if i == 0 and first(b):
                        dve.wait_ge(aggr_d[n], NT * b)
                    dve.bn_stats(stat[n][:, i, :], xs[:, b, i, :]).then_inc(stat_d[n], 1)
                if first(b):
                    dve.wait_ge(veps_d[n], b)
                    dve.wait_ge(nmr_d[n], b)
                for i in range(NT):
                    dve.wait_ge(stat_d[n], NT * b + i + 1)
                    dve.bn_aggr(mv[n][:, i, :], stat[n][:, i, :]).then_inc(aggr_d[n], 1)
                dve.wait_ge(aggr_d[n], NT * (b + 1))
                if first(b):
                    dve.wait_ge(rstd_p[n], b)
                dve.tensor_scalar(veps[n][:, :], mv[n][:, :, 1], EPS, None, ALU.add).then_inc(veps_d[n], 1)

            def mean_rstd(n, b):
                dve.wait_ge(rstd_p[n], b + 1)
                if first(b):
                    dve.wait_ge(xn_p[n], NT * b)
                dve.scalar_tensor_tensor(nmr[n][:, :], mv[n][:, :, 0], -1.0, rstd[n][:, :], ALU.mult,
                                         ALU.mult).then_inc(nmr_d[n], 1)

            def split_h(n, b):
                for k in range(KD):
                    dve.wait_ge(h_full_a[n], KD * b + k + 1)
                    if k == 0 and first(b):
                        dve.wait_ge(sc_pe if n == 0 else s_pe, (NT if n == 0 else 1) * b)
                    dve.tensor_copy(h_hi[n][:, k, :], h_full[n][:, k, :]).then_inc(h_hi_d[n], 1)
                for k in range(KD):
                    dve.wait_ge(h_hi_d[n], KD * b + k + 1)
                    dve.tensor_tensor(h_lo[n][:, k, :], h_full[n][:, k, :], f(h_hi[n][:, k, :]),
                                      ALU.subtract).then_inc(h_lo_d[n], 1)

            def low_t(b, m):
                dve.wait_ge(t_hi_a, KD * b + m + 1)
                dve.tensor_tensor(t_lo[:, m, :], A[m][:, :], f(t_hi[:, m, :]), ALU.subtract).then_inc(t_lo_d, 1)

            def low_v(b, h):
                dve.wait_ge(v_hi_a, 2 * b + h + 1)
                q = slice(HALF * h, HALF * (h + 1))
                dve.tensor_tensor(v_lo[:, q, :], A[h][:, :].rearrange("p (i d) -> p i d", d=D), f(v_hi[:, q, :]),
                                  ALU.subtract).then_inc(v_lo_d, 1)

            def row_max(b, i):
                dve.wait_ge(sc_pe, NT * b + i + 1)
                if first(b):
                    dve.wait_ge(exp_a, NT * (b - 1) + i + 1)
                dve.tensor_reduce(negmax[:, i:i + 1], SC[i % 2][:, 0:(i + 1) * P], AX.X, ALU.max,
                                  negate=True).then_inc(max_d, 1)

            def low_pt(b, g):
                n = pt_hi[g].shape[1]
                dve.wait_ge(pt_hi_a, NG * b + g + 1)
                dve.tensor_tensor(pt_lo[g][:, :, :], C[g % 2][:, 0:n * P].rearrange("p (n q) -> p n q", q=P),
                                  f(pt_hi[g][:, :, :]), ALU.subtract).then_inc(pt_lo_d, 1)

            def recip(b):
                dve.wait_ge(exp_a, NT * (b + 1))
                if first(b):
                    dve.wait_ge(y_d, NT * b)
                dve.reciprocal(rden[:, :], den[:, :]).then_inc(rden_d, 1)

            def weigh(b, h):
                if h == 0 and first(b) is False:
                    dve.wait_ge(gates_in, 16)
                dve.wait_ge(rden_d, b + 1)
                dve.wait_ge(pv_pe, 2 * b + h + 1)
                if first(b):
                    dve.wait_ge(x2_p, 2 * b)
                for n in range(HALF):
                    i = HALF * h + n
                    dve.scalar_tensor_tensor(y[:, i, :], C[1 - h][:, n * D:(n + 1) * D], rden[:, i:i + 1],
                                             gates[:, b, 0, :], ALU.mult, ALU.mult).then_inc(y_d, 1)

            def accumulate(b, j):
                n = NJ * b + j
                dve.wait_ge(relu_a, n + 1)
                if j == 0:
                    if first(b):
                        dve.wait_ge(g_lo_d, b)
                    dve.tensor_scalar(acc[:, :], relu[0][:, :], w2c[:, 0:1], b2c[:, 0:1], ALU.mult,
                                      ALU.add).then_inc(acc_d, 1)
                else:
                    dve.wait_ge(acc_d, n)
                    dve.scalar_tensor_tensor(acc[:, :], relu[j % RING][:, :], w2c[:, j:j + 1], acc[:, :],
                                             ALU.mult, ALU.add).then_inc(acc_d, 1)

            def split_g(b):
                dve.wait_ge(acc_d, NJ * (b + 1))
                if first(b):
                    dve.wait_ge(o_pe, 2 * b)
                dve.tensor_copy(g_hi[:, :], acc[:, :]).then_inc(g_hi_d, 1)
                dve.wait_ge(g_hi_d, b + 1)
                dve.tensor_tensor(g_lo[:, :], acc[:, :], f(g_hi[:, :]), ALU.subtract).then_inc(g_lo_d, 1)

            def finish(b, h):
                dve.wait_ge(o_pe, 2 * b + h + 1)
                q = slice(HALF * h, HALF * (h + 1))
                dve.tensor_tensor(xs[:, b, q, :], E[1 - h][:, :].rearrange("p (i d) -> p i d", d=D), xs[:, b, q, :],
                                  ALU.add).then_inc(fin_d, 1)

            dve.wait_ge(c_exped, 1)
            dve.tensor_scalar(c_den[:, :], c_exp[:, :], 1.0, None, ALU.add).then_inc(c_steps, 1)
            dve.wait_ge(c_steps, 1)
            dve.reciprocal(c_sig[:, :], c_den[:, :]).then_inc(c_steps, 1)
            dve.wait_ge(c_steps, 2)
            dve.tensor_tensor(c_silu[:, :], c_sb[:, :], c_sig[:, :], ALU.mult).then_inc(c_steps, 1)
            statistics(0, 0)
            dve.wait_ge(siluT_pe, 1)
            dve.tensor_copy(siluT[:, :, :], E[0][:, 0:KD * B].rearrange("p (k b) -> p k b", k=KD)).then_inc(siluT_sb, 1)
            mean_rstd(0, 0)

            def mod_columns(n):
                dve.wait_ge(mod_pe, n + 1)
                for q in range(2):
                    o = (2 * n + q) * KD * B
                    ins = dve.tensor_scalar(mod[:, 2 * n + q, :, :], E[1][:, o:o + KD * B].rearrange("p (k b) -> p k b", k=KD),
                                            float(q), None, ALU.add)
                ins.then_inc(mod_sb, 1)

            mod_columns(0)
            dve.wait_ge(m_hi_sb, 1)
            dve.scalar_tensor_tensor(m_lo[:, :, :], C[0][:, :].rearrange("p (k d) -> p k d", k=KD), SCALE,
                                     f(m_hi[:, :, :]), ALU.mult, ALU.subtract).then_inc(m_lo_sb, 1)
            dve.wait_ge(wv_in, 16)
            dve.tensor_copy(wv_hi[:, :, :], wv[:, :, :]).then_inc(w_hi_sb, 1)
            dve.wait_ge(w_hi_sb, 1)
            dve.tensor_tensor(wv_lo[:, :, :], wv[:, :, :], f(wv_hi[:, :, :]), ALU.subtract).then_inc(w_lo_sb, 1)
            mod_columns(1)
            dve.wait_ge(gate_pe, 1)
            rows = C[1][0:B, :].rearrange("b (n d) -> b n d", n=2)
            dve.tensor_scalar(gate_sign[:, :, :], rows, 0.0, 2.0, ALU.is_ge, ALU.mult).then_inc(gate_steps, 1)
            dve.tensor_scalar(gate_abs[:, :, :], rows, GATE_MIN, None, ALU.max).then_inc(gate_steps, 1)
            dve.tensor_scalar(gate_neg[:, :, :], rows, -1.0, GATE_MIN, ALU.mult, ALU.max).then_inc(gate_steps, 1)
            dve.wait_ge(gate_steps, 3)
            dve.tensor_tensor(gate_abs[:, :, :], gate_abs[:, :, :], gate_neg[:, :, :], ALU.max).then_inc(gate_steps, 1)
            dve.wait_ge(gate_steps, 4)
            dve.scalar_tensor_tensor(gate[:, :, :], gate_sign[:, :, :], -1.0, gate_abs[:, :, :], ALU.add,
                                     ALU.mult).then_inc(gate_steps, 1)
            dve.wait_ge(gate_steps, 5)
            dve.wait_ge(bout_in, 16)
            dve.tensor_tensor(boutg[:, :], bout_sb[:, :], gate[:, 1, :], ALU.mult).then_inc(gate_steps, 1)
            dve.wait_ge(gate_steps, 6)
            dve.tensor_copy(boutg_hi[:, :], boutg[:, :]).then_inc(gate_steps, 1)
            dve.wait_ge(gate_steps, 7)
            dve.tensor_tensor(boutg_lo[:, :], boutg[:, :], f(boutg_hi[:, :]), ALU.subtract).then_inc(gate_steps, 1)

            def set_up_ffn():
                dve.wait_ge(win_in, 32)
                win_v = win[:, :, :, :].rearrange("p k r m -> p k (r m)")
                dve.tensor_copy(win_hi[:, :, :], win_v).then_inc(w_hi_sb, 1)
                dve.wait_ge(w_hi_sb, 2)
                dve.tensor_tensor(win_lo[:, :, :], win_v, f(win_hi[:, :, :]), ALU.subtract).then_inc(w_lo_sb, 1)
                dve.wait_ge(small_in, 11 * 16)
                dve.tensor_scalar(relu_bias[:, :], w1c[:, :], binc[:, 0:1], None, ALU.mult).then_inc(rbias, 1)
                dve.wait_ge(rbias, 1)
                dve.tensor_tensor(relu_bias[:, :], relu_bias[:, :], b1c[:, :], ALU.add).then_inc(rbias, 1)

            def step(i, live):
                b = i - 1
                if live(b):
                    row_max(b, 0)
                    row_max(b, 1)
                if live(i - 3):
                    split_g(i - 3)
                if live(b):
                    row_max(b, 2)
                if live(i - 2):
                    statistics(1, i - 2)
                if live(b):
                    row_max(b, 3)
                    recip(b)
                if live(i - 2):
                    mean_rstd(1, i - 2)
                if live(i):
                    split_h(0, i)
                if live(i - 3):
                    finish(i - 3, 0)
                    finish(i - 3, 1)
                if live(i - 2):
                    split_h(1, i - 2)
                if live(b):
                    for g in range(NG):
                        low_pt(b, g)
                if live(i + 1):
                    statistics(0, i + 1)
                if live(i):
                    for m in range(KD):
                        low_t(i, m)
                if live(i + 1):
                    mean_rstd(0, i + 1)
                if live(i - 2):
                    for j in range(3):
                        accumulate(i - 2, j)
                if live(b):
                    weigh(b, 0)
                if live(i - 2):
                    for j in range(3, 5):
                        accumulate(i - 2, j)
                if live(b):
                    weigh(b, 1)
                if live(i - 2):
                    accumulate(i - 2, 5)
                if live(i):
                    low_v(i, 0)
                if live(i - 2):
                    accumulate(i - 2, 6)
                    accumulate(i - 2, 7)
                if live(i):
                    low_v(i, 1)

            set_up_ffn()
            steps(lambda i, live: step(i, live) if i >= 0 else None)


_IN = ["L0_attn_x", "L0_attn_WQ", "L0_attn_WK", "L0_attn_WV", "L0_ffn_Win", "L0_ffn_bin_", "L0_ffn_W1",
       "L0_ffn_b1", "L0_ffn_W2", "L0_ffn_b2", "L0_ffn_Wout", "L0_ffn_bout", "L0_c", "L0_wmod"]


def kernel(**inputs):
    import numpy as np
    import concourse.bacc as bacc
    from concourse.bass_utils import run_bass_kernel_spmd

    nc = bacc.Bacc("TRN2", target_bir_lowering=False, num_devices=1)
    arrays, args = {}, []
    for name in _IN:
        a = np.ascontiguousarray(inputs[name])
        arrays[name] = a
        args.append(nc.dram_tensor(name, a.shape, mybir.dt.from_np(a.dtype), kind="ExternalInput").ap())
    out = nc.dram_tensor("out", arrays["L0_attn_x"].shape, mybir.dt.float32, kind="ExternalOutput").ap()
    adaln_layer(nc, *args, out)
    return run_bass_kernel_spmd(nc, [arrays], core_ids=[0]).results[0]["out"]
```

```python
import concourse.bass as bass
from concourse import mybir
from contextlib import ExitStack


def adaln_layer(nc, x, WQ, WK, WV, Win, bin_, W1, b1, W2, b2, Wout, bout, c, wmod, out):
    fp32, fp32r, bf16 = mybir.dt.float32, mybir.dt.float32r, mybir.dt.bfloat16
    ALU, ACT, AX = mybir.AluOpType, mybir.ActivationFunctionType, mybir.AxisListType

    B, S, D = x.shape
    P = 128
    NT = S // P
    KD = D // P
    M, INNER = W1.shape
    NJ = INNER // 2
    HALF = NT // 2
    SCALE = float(D) ** -0.5
    EPS = 1e-5
    GATE_MIN = 0.25
    MASKED = -1.0e38
    SA, CA, GA, SB, CB, GB = range(6)
    MIN_N = 256
    RING = 8

    ctx = ExitStack()
    with ctx:
        def sb(name, shape, dt=fp32):
            return ctx.enter_context(nc.sbuf_tensor(name, shape, dt))

        def sem(name):
            return ctx.enter_context(nc.semaphore(name))

        def f(ap):
            return ap.bitcast(fp32)

        ident = sb("ident", [P, P])
        ident_bf = sb("ident_bf", [P, P], bf16)
        mask_bf = sb("mask_bf", [P, P], bf16)
        minus_half = sb("minus_half", [P, NT])
        ones2 = sb("ones2", [2, P], fp32r)
        wq = sb("wq", [P, KD, D])
        wk = sb("wk", [P, KD, D])
        wqT = sb("wqT", [P, KD, D])
        wkT = sb("wkT", [P, KD, D])
        m_hi = sb("m_hi", [P, KD, D], fp32r)
        m_lo = sb("m_lo", [P, KD, D], fp32r)
        wv = sb("wv", [P, KD, D])
        wv_hi = sb("wv_hi", [P, KD, D], fp32r)
        wv_lo = sb("wv_lo", [P, KD, D], fp32r)
        win = sb("win", [P, KD, 2, M])
        wout = sb("wout", [P, D])
        w1c = sb("w1c", [P, NJ])
        b1c = sb("b1c", [P, NJ])
        w2c = sb("w2c", [P, NJ])
        b2c = sb("b2c", [P, 1])
        binc = sb("binc", [P, 1])
        relu_bias = sb("relu_bias", [P, NJ])
        c_sb = sb("c_sb", [B, D])
        c_exp = sb("c_exp", [B, D])
        c_den = sb("c_den", [B, D])
        c_sig = sb("c_sig", [B, D])
        c_silu = sb("c_silu", [B, D])
        siluT = sb("siluT", [P, KD, B])
        wmod_sb = sb("wmod_sb", [P, KD, 6, D])
        mod = sb("mod", [P, 4, KD, B])
        gate_sign = sb("gate_sign", [B, 2, D])
        gate_abs = sb("gate_abs", [B, 2, D])
        gate_neg = sb("gate_neg", [B, 2, D])
        gate = sb("gate", [B, 2, D])
        bout_sb = sb("bout_sb", [B, D])
        boutg = sb("boutg", [B, D])
        boutg_hi = sb("boutg_hi", [B, D], fp32r)
        boutg_lo = sb("boutg_lo", [B, D], fp32r)
        gates = sb("gates", [P, B, 2, D])
        bout2 = sb("bout2", [2, B, D], fp32r)
        xs = sb("xs", [P, B, NT, D])
        stat = [sb(f"stat{n}", [P, NT, 6]) for n in (1, 2)]
        mv = [sb(f"mv{n}", [P, NT, 2]) for n in (1, 2)]
        veps = [sb(f"veps{n}", [P, NT]) for n in (1, 2)]
        rstd = [sb(f"rstd{n}", [P, NT]) for n in (1, 2)]
        negmean = [sb(f"negmean{n}", [P, NT]) for n in (1, 2)]
        xn = [sb(f"xn{n}", [P, NT, D]) for n in (1, 2)]
        h_full = [sb(f"h_full{n}", [P, KD, S]) for n in (1, 2)]
        h_hi = sb("h_hi", [P, KD, S], fp32r)
        h_lo = sb("h_lo", [P, KD, S], fp32r)
        t_hi = sb("t_hi", [P, KD, S], fp32r)
        t_lo = sb("t_lo", [P, KD, S], fp32r)
        v_hi = sb("v_hi", [P, NT, D], fp32r)
        v_lo = sb("v_lo", [P, NT, D], fp32r)
        negmax = sb("negmax", [P, NT])
        den = sb("den", [P, NT])
        rden = sb("rden", [P, NT])
        probs = [sb(f"probs{i}", [P, (i + 1) * P]) for i in range(NT)]
        GROUPS = [[0, 1], [2], [3]]
        pt_hi = [sb(f"pt_hi{g}", [P, sum(i + 1 for i in q), P], fp32r) for g, q in enumerate(GROUPS)]
        pt_lo = [sb(f"pt_lo{g}", [P, sum(i + 1 for i in q), P], fp32r) for g, q in enumerate(GROUPS)]
        NG = len(GROUPS)
        y = sb("y", [P, NT, D])
        ffn = sb("ffn", [P, NT, D])
        relu = [sb(f"relu{k}", [P, S]) for k in range(RING)]
        acc = sb("acc", [P, S])
        wog = sb("wog", [P, D])

        def pt_slot(i, j):
            g = next(n for n, q in enumerate(GROUPS) if i in q)
            return g, sum(k + 1 for k in GROUPS[g] if k < i) + j

        def bank(name):
            return ctx.enter_context(nc.psum_tensor(name, [P, S], fp32))

        A = [bank("A0"), bank("A1")]
        SC = [bank("B0"), bank("B1")]
        C = [bank("C0"), bank("C1")]
        E = [bank("D0"), bank("D1")]

        gate_dram = nc.dram_tensor("gate_scratch", [B, 2 * D], fp32)
        bout_dram = nc.dram_tensor("bout_scratch", [2, B, D], fp32)

        c_in, wmod_in, wmod2_in = sem("c_in"), sem("wmod_in"), sem("wmod2_in")
        wqk_in, wv_in, win_in, small_in, bout_in = sem("wqk_in"), sem("wv_in"), sem("win_in"), sem("small_in"), sem("bout_in")
        consts, b2_zero = sem("consts"), sem("b2_zero")
        c_exped, c_steps, siluT_pe, siluT_sb = sem("c_exped"), sem("c_steps"), sem("siluT_pe"), sem("siluT_sb")
        wT_pe, wT_sb, m_pe, m_hi_sb, m_lo_sb = sem("wT_pe"), sem("wT_sb"), sem("m_pe"), sem("m_hi_sb"), sem("m_lo_sb")
        w_hi_sb, w_lo_sb = sem("w_hi_sb"), sem("w_lo_sb")
        mod_pe, mod_sb, gate_pe, gate_steps = sem("mod_pe"), sem("mod_sb"), sem("gate_pe"), sem("gate_steps")
        gate_out, bout_out, gates_in, bout2_in = sem("gate_out"), sem("bout_out"), sem("gates_in"), sem("bout2_in")
        rbias = sem("rbias")
        x_in = sem("x_in")
        stat_d = [sem(f"stat_d{n}") for n in (1, 2)]
        aggr_d = [sem(f"aggr_d{n}") for n in (1, 2)]
        veps_d = [sem(f"veps_d{n}") for n in (1, 2)]
        rstd_p = [sem(f"rstd_p{n}") for n in (1, 2)]
        negmean_d = [sem(f"negmean_d{n}") for n in (1, 2)]
        xn_p = [sem(f"xn_p{n}") for n in (1, 2)]
        xT_pe = [sem(f"xT_pe{n}") for n in (1, 2)]
        h_full_a = [sem(f"h_full_a{n}") for n in (1, 2)]
        h_hi_a, h_lo_d = sem("h_hi_a"), sem("h_lo_d")
        t_pe, t_hi_a, t_lo_d = sem("t_pe"), sem("t_hi_a"), sem("t_lo_d")
        v_pe, v_hi_a, v_lo_d = sem("v_pe"), sem("v_hi_a"), sem("v_lo_d")
        sc_pe, max_d, exp_a = sem("sc_pe"), sem("max_d"), sem("exp_a")
        pt_pe, pt_hi_a, pt_lo_d = sem("pt_pe"), sem("pt_hi_a"), sem("pt_lo_d")
        rden_d, pv_pe, y_d, x2_p = sem("rden_d"), sem("pv_pe"), sem("y_d"), sem("x2_p")
        s_pe, relu_a, acc_d = sem("s_pe"), sem("relu_a"), sem("acc_d")
        wog_p = sem("wog_p")
        o_pe, ffn_a, fin_p, stored = sem("o_pe"), sem("ffn_a"), sem("fin_p"), sem("stored")

        block = ctx.enter_context(nc.Block())

        LAST_LAG = 3

        def steps(step):
            for i in range(-1, B + LAST_LAG):
                step(i, lambda b: 0 <= b < B)

        @block.sync
        def _(sp):
            x_v = x.rearrange("b (i p) d -> p b i d", p=P)
            out_v = out.rearrange("b (i p) d -> p b i d", p=P)

            def load(b):
                sp.dma_start(xs[:, b, :, :], x_v[:, b, :, :]).then_inc(x_in, 16)

            def store(b, h):
                sp.wait_ge(fin_p, 2 * b + h + 1)
                sp.dma_start(out_v[:, b, HALF * h:HALF * (h + 1), :],
                             xs[:, b, HALF * h:HALF * (h + 1), :]).then_inc(stored, 16)

            load(0)
            sp.dma_start(wq[:, :, :], WQ.rearrange("(k p) e -> p k e", p=P)).then_inc(wqk_in, 16)
            sp.dma_start(wk[:, :, :], WK.rearrange("(k p) e -> p k e", p=P)).then_inc(wqk_in, 16)
            sp.dma_start(wv[:, :, :], WV.rearrange("(k p) e -> p k e", p=P)).then_inc(wv_in, 16)
            for r in range(2):
                sp.dma_start(win[:, :, r, :], Win.rearrange("(k p) m -> p k m", p=P)).then_inc(win_in, 16)
            sp.wait_ge(b2_zero, 1)
            for r in range(2):
                q = slice(r * M, (r + 1) * M)
                sp.dma_start(w1c[q, :], W1[:, r * NJ:(r + 1) * NJ]).then_inc(small_in, 16)
                sp.dma_start(b1c[q, :], b1[:, r * NJ:(r + 1) * NJ]).then_inc(small_in, 16)
                sp.dma_start(w2c[q, :], W2[:, r * NJ:(r + 1) * NJ]).then_inc(small_in, 16)
                sp.dma_start(binc[q, :], bin_.rearrange("(m a) -> m a", a=1)).then_inc(small_in, 16)
                sp.dma_start(wout[q, :], Wout[:, :]).then_inc(small_in, 16)
            sp.dma_start(b2c[0:M, :], b2.rearrange("(m a) -> m a", a=1)).then_inc(small_in, 16)
            sp.wait_ge(x_in, 16)
            load(1)
            sp.wait_ge(gate_steps, 5)
            sp.dma_start(gate_dram[:, :], gate[:, :, :].rearrange("b n d -> b (n d)")).then_inc(gate_out, 16)
            sp.wait_ge(gate_out, 16)
            sp.dma_start(gates[:, :, :, :].rearrange("p b n d -> p (b n d)"),
                         gate_dram[:, :].rearrange("b n -> (b n)").partition_broadcast(P)).then_inc(gates_in, 16)
            sp.wait_ge(gate_steps, 8)
            sp.dma_start(bout_dram[0, :, :], f(boutg_hi[:, :])).then_inc(bout_out, 16)
            sp.dma_start(bout_dram[1, :, :], f(boutg_lo[:, :])).then_inc(bout_out, 16)
            sp.wait_ge(bout_out, 32)
            sp.dma_start(f(bout2[:, :, :]), bout_dram[:, :, :]).then_inc(bout2_in, 16)

            def step(i, live):
                if live(i + 2):
                    sp.wait_ge(x_in, 16 * (i + 2))
                    load(i + 2)
                if live(i - 3):
                    store(i - 3, 0)
                    store(i - 3, 1)

            steps(lambda i, live: step(i, live) if i >= 0 else None)
            sp.wait_ge(stored, 2 * B * 16)

        @block.gpsimd
        def _(pool):
            pool.memset(b2c[:, :], 0.0).then_inc(b2_zero, 1)
            pool.memset(ident[:, :], 0.0).then_inc(consts, 1)
            pool.memset(mask_bf[:, :], 0.0).then_inc(consts, 1)
            pool.memset(minus_half[:, :], -0.5).then_inc(consts, 1)
            pool.memset(f(ones2[:, :]), 1.0).then_inc(consts, 1)
            pool.memset(ident_bf[:, :], 0.0).then_inc(consts, 1)
            pool.wait_ge(consts, 5)
            for m in (ident, ident_bf):
                pool.affine_select(out=m[:, :], in_=m[:, :], compare_op=ALU.not_equal, fill=1.0, base=0,
                                   pattern=[[-1, P]], channel_multiplier=1).then_inc(consts, 1)
            pool.affine_select(out=mask_bf[:, :], in_=mask_bf[:, :], compare_op=ALU.is_ge, fill=MASKED, base=0,
                               pattern=[[-1, P]], channel_multiplier=1).then_inc(consts, 1)

            def rsqrt(n, b):
                pool.wait_ge(veps_d[n], b + 1)
                if first(b):
                    pool.wait_ge(xn_p[n], NT * b)
                pool.tensor_tensor(rstd[n][:, :], veps[n][:, :], minus_half[:, :], ALU.pow).then_inc(rstd_p[n], 1)

            def normalise(n, b):
                pool.wait_ge(negmean_d[n], b + 1)
                pool.wait_ge(rstd_p[n], b + 1)
                if first(b):
                    pool.wait_ge(xT_pe[n], KD * b)
                for i in range(NT):
                    pool.tensor_scalar(xn[n][:, i, :], xs[:, b, i, :], negmean[n][:, i:i + 1], rstd[n][:, i:i + 1],
                                       ALU.add, ALU.mult).then_inc(xn_p[n], 1)

            def first(b):
                return not (isinstance(b, int) and b == 0)

            def gate_wout(b):
                if not first(b):
                    pool.wait_ge(small_in, 11 * 16)
                    pool.wait_ge(gates_in, 16)
                if first(b):
                    pool.wait_ge(o_pe, 2 * b)
                pool.tensor_tensor(wog[:, :], wout[:, :], gates[:, b, 1, :], ALU.mult).then_inc(wog_p, 1)

            def add_attention(b, h):
                pool.wait_ge(y_d, NT * b + HALF * (h + 1))
                q = slice(HALF * h, HALF * (h + 1))
                pool.tensor_tensor(xs[:, b, q, :], xs[:, b, q, :], y[:, q, :], ALU.add).then_inc(x2_p, 1)

            def finish(b, h):
                pool.wait_ge(ffn_a, 2 * b + h + 1)
                q = slice(HALF * h, HALF * (h + 1))
                pool.tensor_tensor(xs[:, b, q, :], xs[:, b, q, :], ffn[:, q, :], ALU.add).then_inc(fin_p, 1)

            def start_sum(b):
                if not first(b):
                    pool.wait_ge(small_in, 11 * 16)
                pool.wait_ge(relu_a, NJ * b + 1)
                if first(b):
                    pool.wait_ge(o_pe, 2 * b)
                pool.tensor_scalar(acc[:, :], relu[0][:, :], w2c[:, 0:1], b2c[:, 0:1], ALU.mult,
                                   ALU.add).then_inc(acc_d, 1)

            def step(i, live):
                if live(i - 2):
                    add_attention(i - 2, 1)
                if live(i - 3):
                    gate_wout(i - 3)
                if live(i - 2):
                    rsqrt(1, i - 2)
                    normalise(1, i - 2)
                if live(i + 1):
                    rsqrt(0, i + 1)
                if live(i - 3):
                    finish(i - 3, 0)
                    finish(i - 3, 1)
                if live(i - 2):
                    start_sum(i - 2)
                if live(i - 1):
                    add_attention(i - 1, 0)
                if live(i + 1):
                    normalise(0, i + 1)

            steps(step)

        @block.scalar
        def _(act):
            act.dma_start(c_sb[:, :], c).then_inc(c_in, 16)
            wm = wmod.rearrange("(k p) (q d) -> p k q d", p=P, d=D)
            act.dma_start(wmod_sb[:, :, SA:CA + 1, :], wm[:, :, SA:CA + 1, :]).then_inc(wmod_in, 16)
            act.dma_start(wmod_sb[:, :, GA:GB + 1, :], wm[:, :, GA:GB + 1, :]).then_inc(wmod2_in, 16)
            act.dma_start(bout_sb[:, :], bout.partition_broadcast(B)).then_inc(bout_in, 16)
            act.wait_ge(c_in, 16)
            act.activation(c_exp[:, :], c_sb[:, :], ACT.Exp, scale=-1.0).then_inc(c_exped, 1)
            for n, dst in enumerate((wqT, wkT)):
                act.wait_ge(wT_pe, n + 1)
                act.activation(dst[:, :, :], SC[n][:, :].rearrange("p (k d) -> p k d", k=KD), ACT.Copy).then_inc(wT_sb, 1)
            act.wait_ge(m_pe, 1)
            act.activation(m_hi[:, :, :], C[0][:, :].rearrange("p (k d) -> p k d", k=KD), ACT.Copy,
                           scale=SCALE).then_inc(m_hi_sb, 1)

            def modulate(n, b):
                for k in range(KD):
                    act.wait_ge(xT_pe[n], KD * b + k + 1)
                    if n == 0 and first(b) is False and k == 0:
                        act.wait_ge(mod_sb, 1)
                    if n == 1 and first(b) is False and k == 0:
                        act.wait_ge(mod_sb, 2)
                    if first(b) and k == 0:
                        act.wait_ge(h_lo_d if n == 0 else s_pe, (KD if n == 0 else 1) * b)
                    act.activation(h_full[n][:, k, :], (A, E)[n][k][:, :], ACT.Identity,
                                   bias=mod[:, 2 * n, k, b:b + 1],
                                   scale=mod[:, 2 * n + 1, k, b:b + 1]).then_inc(h_full_a[n], 1)

            def first(b):
                return not (isinstance(b, int) and b == 0)

            def round_h(b, k):
                if k == 0 and first(b):
                    act.wait_ge(sc_pe, NT * b)
                    act.wait_ge(v_pe, 2 * b)
                act.wait_ge(h_full_a[0], KD * b + k + 1)
                act.activation(h_hi[:, k, :], h_full[0][:, k, :], ACT.Copy).then_inc(h_hi_a, 1)

            def exps(b, i):
                act.wait_ge(max_d, NT * b + i + 1)
                if first(b):
                    act.wait_ge(pt_pe, NG * b)
                    act.wait_ge(rden_d, b)
                act.activation(probs[i][:, :], SC[i % 2][:, 0:(i + 1) * P], ACT.Exp, bias=negmax[:, i:i + 1],
                               accum_out=den[:, i:i + 1]).then_inc(exp_a, 1)

            def round_pt(b, g):
                n = pt_hi[g].shape[1]
                act.wait_ge(pt_pe, NG * b + g + 1)
                if first(b):
                    act.wait_ge(pv_pe, 2 * b)
                act.activation(pt_hi[g][:, :, :], C[g % 2][:, 0:n * P].rearrange("p (n q) -> p n q", q=P),
                               ACT.Copy).then_inc(pt_hi_a, 1)

            def round_t(b, m):
                act.wait_ge(t_pe, KD * b + m + 1)
                if first(b):
                    act.wait_ge(sc_pe, NT * b)
                act.activation(t_hi[:, m, :], A[m][:, :], ACT.Copy).then_inc(t_hi_a, 1)

            def round_v(b, h):
                act.wait_ge(v_pe, 2 * b + h + 1)
                if first(b):
                    act.wait_ge(pv_pe, 2 * b)
                act.activation(v_hi[:, HALF * h:HALF * (h + 1), :], A[h][:, :].rearrange("p (i d) -> p i d", d=D),
                               ACT.Copy).then_inc(v_hi_a, 1)

            def copy_ffn(b, h):
                act.wait_ge(o_pe, 2 * b + h + 1)
                if first(b):
                    act.wait_ge(fin_p, 2 * (b - 1) + h + 1)
                act.activation(ffn[:, HALF * h:HALF * (h + 1), :], E[1 - h][:, :].rearrange("p (i d) -> p i d", d=D),
                               ACT.Copy).then_inc(ffn_a, 1)

            def relus(b, j):
                if j == 0:
                    act.wait_ge(s_pe, b + 1)
                    if not first(b):
                        act.wait_ge(rbias, 2)
                n = NJ * b + j
                if first(b) or j >= RING:
                    act.wait_ge(acc_d, n - RING + 1)
                act.activation(relu[j % RING][:, :], E[0][:, :], ACT.Relu, bias=relu_bias[:, j:j + 1],
                               scale=w1c[:, j:j + 1]).then_inc(relu_a, 1)

            def step(i, live):
                if live(i - 3):
                    relus(i - 3, 4)
                if live(i - 1):
                    exps(i - 1, 0)
                if live(i - 3):
                    relus(i - 3, 5)
                if live(i - 1):
                    exps(i - 1, 1)
                if live(i - 3):
                    relus(i - 3, 6)
                if live(i - 1):
                    round_v(i - 1, 0)
                if live(i - 3):
                    relus(i - 3, 7)
                if live(i - 1):
                    exps(i - 1, 2)
                    round_v(i - 1, 1)
                    exps(i - 1, 3)
                    round_pt(i - 1, 0)
                    round_pt(i - 1, 1)
                if live(i):
                    modulate(0, i)
                    round_h(i, 0)
                if live(i - 3):
                    copy_ffn(i - 3, 0)
                if live(i):
                    round_h(i, 1)
                if live(i - 3):
                    copy_ffn(i - 3, 1)
                if live(i - 1):
                    round_pt(i - 1, 2)
                if live(i - 2):
                    modulate(1, i - 2)
                if live(i):
                    round_t(i, 0)
                if live(i - 2):
                    relus(i - 2, 0)
                    relus(i - 2, 1)
                if live(i):
                    round_t(i, 1)
                if live(i - 2):
                    relus(i - 2, 2)
                    relus(i - 2, 3)

            steps(step)

        @block.tensor
        def _(pe):
            def three(dst, lhs, rhs, parts, inc=None, open_=False):
                n = len(parts)
                for q, part in enumerate(parts):
                    lh, ll, rh, rl = lhs[0](part), lhs[1](part), rhs[0](part), rhs[1](part)
                    pe.matmul(dst, ll, rh, start=(q == 0), stop=False)
                    pe.matmul(dst, lh, rl, start=False, stop=False)
                    mm = pe.matmul(dst, lh, rh, start=False, stop=(q == n - 1 and not open_))
                return mm

            def first(b):
                return not (isinstance(b, int) and b == 0)

            pe.wait_ge(consts, 8)
            pe.wait_ge(wqk_in, 32)
            for n, w in enumerate((wq, wk)):
                for e in range(KD):
                    for d in range(KD):
                        mm = pe.transpose(SC[n][:, e * D + d * P:e * D + (d + 1) * P],
                                          w[:, d, e * P:(e + 1) * P], ident[:, :])
                mm.then_inc(wT_pe, 1)
            pe.wait_ge(c_steps, 3)
            for k in range(KD):
                mm = pe.transpose(E[0][:, k * B:(k + 1) * B], c_silu[:, k * P:(k + 1) * P], ident[0:B, 0:B])
            mm.then_inc(siluT_pe, 1)
            pe.wait_ge(wT_sb, 2)
            for d in range(KD):
                for e in range(KD):
                    mm = pe.matmul(C[0][:, d * D:(d + 1) * D], wqT[:, e, d * P:(d + 1) * P], wkT[:, e, :],
                                   start=(e == 0), stop=(e == KD - 1))
            mm.then_inc(m_pe, 1)
            pe.wait_ge(siluT_sb, 1)

            def modulation(n, qs):
                for q, which in enumerate(qs):
                    for k in range(KD):
                        for e in range(KD):
                            col = ((2 * n + q) * KD + k) * B
                            mm = pe.matmul(E[1][:, col:col + B], wmod_sb[:, e, which, k * P:(k + 1) * P],
                                           siluT[:, e, :], start=(e == 0), stop=(e == KD - 1))
                mm.then_inc(mod_pe, 1)

            def transpose_x(n, b):
                pe.wait_ge(xn_p[n], NT * (b + 1))
                if n == 0 and first(b):
                    pe.wait_ge(v_lo_d, 2 * b)
                if n == 1:
                    pe.wait_ge(mod_sb, 2)
                    if first(b):
                        pe.wait_ge(ffn_a, 2 * b)
                for k in range(KD):
                    for i in range(NT):
                        mm = pe.transpose((A, E)[n][k][:, i * P:(i + 1) * P], xn[n][:, i, k * P:(k + 1) * P], ident[:, :])
                    mm.then_inc(xT_pe[n], 1)

            def project_t(b, m):
                if not first(b):
                    pe.wait_ge(m_lo_sb, 1)
                pe.wait_ge(h_lo_d, KD * (b + 1))
                three(A[m][:, :],
                      [lambda k, w=w: w[:, k, m * P:(m + 1) * P] for w in (m_hi, m_lo)],
                      [lambda k, w=w: w[:, k, :] for w in (h_hi, h_lo)], range(KD)).then_inc(t_pe, 1)

            def project_v(b, h):
                if not first(b):
                    pe.wait_ge(w_lo_sb, 1)
                pe.wait_ge(t_lo_d, KD * b + h + 1)
                for n in range(HALF):
                    i = HALF * h + n
                    mm = three(A[h][:, n * D:(n + 1) * D],
                               [lambda k, w=w, i=i: w[:, k, i * P:(i + 1) * P] for w in (h_hi, h_lo)],
                               [lambda k, w=w: w[:, k, :] for w in (wv_hi, wv_lo)], range(KD))
                mm.then_inc(v_pe, 1)

            def scores(b, i):
                if i == 0:
                    pe.wait_ge(t_lo_d, KD * (b + 1))
                if first(b) or i >= 2:
                    pe.wait_ge(exp_a, NT * b + i - 1)
                width = max((i + 1) * P, MIN_N)
                dst = SC[i % 2]
                three(dst[:, 0:width],
                      [lambda k, w=w: w[:, k, i * P:(i + 1) * P] for w in (t_hi, t_lo)],
                      [lambda k, w=w: w[:, k, 0:width] for w in (h_hi, h_lo)], range(KD), open_=True)
                pe.matmul(dst[:, i * P:(i + 1) * P], ident_bf[:, :], mask_bf[:, :], start=False,
                          stop=True).then_inc(sc_pe, 1)

            def transpose_p(b, g):
                pe.wait_ge(exp_a, NT * b + GROUPS[g][-1] + 1)
                if g < 2:
                    if first(b):
                        pe.wait_ge(y_d, NT * b)
                else:
                    pe.wait_ge(pt_lo_d, NG * b + 1)
                for i in GROUPS[g]:
                    for j in range(i + 1):
                        s = pt_slot(i, j)[1]
                        mm = pe.transpose(C[g % 2][:, s * P:(s + 1) * P], probs[i][:, j * P:(j + 1) * P], ident[:, :])
                mm.then_inc(pt_pe, 1)

            def attend(b, h):
                pe.wait_ge(pt_lo_d, NG * b + 2 + h)
                pe.wait_ge(v_lo_d, 2 * b + 1 + h)
                for n in range(HALF):
                    i = HALF * h + n
                    g = pt_slot(i, 0)[0]
                    mm = three(C[1 - h][:, n * D:(n + 1) * D],
                               [lambda j, w=w: w[g][:, pt_slot(i, j)[1], :] for w in (pt_hi, pt_lo)],
                               [lambda j, w=w: w[:, j, :] for w in (v_hi, v_lo)], range(i + 1))
                mm.then_inc(pv_pe, 1)

            def hidden(b):
                if not first(b):
                    pe.wait_ge(win_in, 32)
                pe.wait_ge(h_full_a[1], KD * (b + 1))
                for k in range(KD):
                    mm = pe.matmul(E[0][:, :], win[:, k, :, :].rearrange("p r m -> p (r m)"), h_full[1][:, k, :],
                                   start=(k == 0), stop=(k == KD - 1))
                mm.then_inc(s_pe, 1)

            def output(b, h):
                if h == 0:
                    pe.wait_ge(acc_d, NJ * (b + 1))
                    pe.wait_ge(wog_p, b + 1)
                    if not first(b):
                        pe.wait_ge(bout2_in, 16)
                for n in range(HALF):
                    i = HALF * h + n
                    dst = E[1 - h][:, n * D:(n + 1) * D]
                    pe.matmul(dst, acc[:, i * P:(i + 1) * P], wog[:, :], start=True, stop=False)
                    mm = pe.matmul(dst, ones2[:, :], bout2[:, b, :], start=False, stop=True)
                mm.then_inc(o_pe, 1)

            def set_up_rest():
                pe.wait_ge(wmod2_in, 16)
                pe.wait_ge(mod_sb, 1)
                modulation(1, (SB, CB))
                for n, which in enumerate((GA, GB)):
                    for e in range(KD):
                        mm = pe.matmul(C[1][0:B, n * D:(n + 1) * D], siluT[:, e, :], wmod_sb[:, e, which, :],
                                       start=(e == 0), stop=(e == KD - 1))
                mm.then_inc(gate_pe, 1)

            def step(i, live):
                if live(i - 1):
                    scores(i - 1, 0)
                    scores(i - 1, 1)
                    project_v(i - 1, 0)
                    scores(i - 1, 2)
                    project_v(i - 1, 1)
                    scores(i - 1, 3)
                    transpose_p(i - 1, 0)
                    transpose_p(i - 1, 1)
                if live(i):
                    transpose_x(0, i)
                if live(i - 3):
                    output(i - 3, 0)
                    output(i - 3, 1)
                if live(i - 1):
                    transpose_p(i - 1, 2)
                    attend(i - 1, 0)
                if live(i - 2):
                    transpose_x(1, i - 2)
                if live(i):
                    project_t(i, 0)
                if live(i - 2):
                    hidden(i - 2)
                if live(i):
                    project_t(i, 1)
                if live(i - 1):
                    attend(i - 1, 1)

            pe.wait_ge(wmod_in, 16)
            modulation(0, (SA, CA))
            set_up_rest()
            steps(step)

        @block.vector
        def _(dve):
            def first(b):
                return not (isinstance(b, int) and b == 0)

            def statistics(n, b):
                for i in range(NT):
                    if n == 0:
                        if i == 0:
                            dve.wait_ge(x_in, 16 * (b + 1))
                    elif i % HALF == 0:
                        dve.wait_ge(x2_p, 2 * b + i // HALF + 1)
                    if i == 0 and first(b):
                        dve.wait_ge(aggr_d[n], NT * b)
                    dve.bn_stats(stat[n][:, i, :], xs[:, b, i, :]).then_inc(stat_d[n], 1)
                if first(b):
                    dve.wait_ge(veps_d[n], b)
                    dve.wait_ge(negmean_d[n], b)
                for i in range(NT):
                    dve.wait_ge(stat_d[n], NT * b + i + 1)
                    dve.bn_aggr(mv[n][:, i, :], stat[n][:, i, :]).then_inc(aggr_d[n], 1)
                dve.wait_ge(aggr_d[n], NT * (b + 1))
                if first(b):
                    dve.wait_ge(rstd_p[n], b)
                dve.tensor_scalar(veps[n][:, :], mv[n][:, :, 1], EPS, None, ALU.add).then_inc(veps_d[n], 1)
                if first(b):
                    dve.wait_ge(xn_p[n], NT * b)
                dve.tensor_scalar(negmean[n][:, :], mv[n][:, :, 0], -1.0, None, ALU.mult).then_inc(negmean_d[n], 1)

            def low_h(b, k):
                dve.wait_ge(h_hi_a, KD * b + k + 1)
                dve.tensor_tensor(h_lo[:, k, :], h_full[0][:, k, :], f(h_hi[:, k, :]),
                                  ALU.subtract).then_inc(h_lo_d, 1)

            def low_t(b, m):
                dve.wait_ge(t_hi_a, KD * b + m + 1)
                dve.tensor_tensor(t_lo[:, m, :], A[m][:, :], f(t_hi[:, m, :]), ALU.subtract).then_inc(t_lo_d, 1)

            def low_v(b, h):
                dve.wait_ge(v_hi_a, 2 * b + h + 1)
                q = slice(HALF * h, HALF * (h + 1))
                dve.tensor_tensor(v_lo[:, q, :], A[h][:, :].rearrange("p (i d) -> p i d", d=D), f(v_hi[:, q, :]),
                                  ALU.subtract).then_inc(v_lo_d, 1)

            def row_max(b, i):
                dve.wait_ge(sc_pe, NT * b + i + 1)
                if first(b):
                    dve.wait_ge(exp_a, NT * (b - 1) + i + 1)
                dve.tensor_reduce(negmax[:, i:i + 1], SC[i % 2][:, 0:(i + 1) * P], AX.X, ALU.max,
                                  negate=True).then_inc(max_d, 1)

            def low_pt(b, g):
                n = pt_hi[g].shape[1]
                dve.wait_ge(pt_hi_a, NG * b + g + 1)
                dve.tensor_tensor(pt_lo[g][:, :, :], C[g % 2][:, 0:n * P].rearrange("p (n q) -> p n q", q=P),
                                  f(pt_hi[g][:, :, :]), ALU.subtract).then_inc(pt_lo_d, 1)

            def recip(b):
                dve.wait_ge(exp_a, NT * (b + 1))
                if first(b):
                    dve.wait_ge(y_d, NT * b)
                dve.reciprocal(rden[:, :], den[:, :]).then_inc(rden_d, 1)

            def weigh(b, h):
                if h == 0 and first(b) is False:
                    dve.wait_ge(gates_in, 16)
                dve.wait_ge(rden_d, b + 1)
                dve.wait_ge(pv_pe, 2 * b + h + 1)
                if first(b):
                    dve.wait_ge(x2_p, 2 * b)
                for n in range(HALF):
                    i = HALF * h + n
                    dve.scalar_tensor_tensor(y[:, i, :], C[1 - h][:, n * D:(n + 1) * D], rden[:, i:i + 1],
                                             gates[:, b, 0, :], ALU.mult, ALU.mult).then_inc(y_d, 1)

            def accumulate(b, j):
                n = NJ * b + j
                dve.wait_ge(relu_a, n + 1)
                dve.wait_ge(acc_d, n)
                dve.scalar_tensor_tensor(acc[:, :], relu[j % RING][:, :], w2c[:, j:j + 1], acc[:, :],
                                         ALU.mult, ALU.add).then_inc(acc_d, 1)

            dve.wait_ge(c_exped, 1)
            dve.tensor_scalar(c_den[:, :], c_exp[:, :], 1.0, None, ALU.add).then_inc(c_steps, 1)
            dve.wait_ge(c_steps, 1)
            dve.reciprocal(c_sig[:, :], c_den[:, :]).then_inc(c_steps, 1)
            dve.wait_ge(c_steps, 2)
            dve.tensor_tensor(c_silu[:, :], c_sb[:, :], c_sig[:, :], ALU.mult).then_inc(c_steps, 1)
            statistics(0, 0)
            dve.wait_ge(siluT_pe, 1)
            dve.tensor_copy(siluT[:, :, :], E[0][:, 0:KD * B].rearrange("p (k b) -> p k b", k=KD)).then_inc(siluT_sb, 1)

            def mod_columns(n):
                dve.wait_ge(mod_pe, n + 1)
                for q in range(2):
                    o = (2 * n + q) * KD * B
                    ins = dve.tensor_scalar(mod[:, 2 * n + q, :, :], E[1][:, o:o + KD * B].rearrange("p (k b) -> p k b", k=KD),
                                            float(q), None, ALU.add)
                ins.then_inc(mod_sb, 1)

            mod_columns(0)
            dve.wait_ge(m_hi_sb, 1)
            dve.scalar_tensor_tensor(m_lo[:, :, :], C[0][:, :].rearrange("p (k d) -> p k d", k=KD), SCALE,
                                     f(m_hi[:, :, :]), ALU.mult, ALU.subtract).then_inc(m_lo_sb, 1)
            dve.wait_ge(wv_in, 16)
            dve.tensor_copy(wv_hi[:, :, :], wv[:, :, :]).then_inc(w_hi_sb, 1)
            dve.wait_ge(w_hi_sb, 1)
            dve.tensor_tensor(wv_lo[:, :, :], wv[:, :, :], f(wv_hi[:, :, :]), ALU.subtract).then_inc(w_lo_sb, 1)
            mod_columns(1)
            dve.wait_ge(gate_pe, 1)
            rows = C[1][0:B, :].rearrange("b (n d) -> b n d", n=2)
            dve.tensor_scalar(gate_sign[:, :, :], rows, 0.0, 2.0, ALU.is_ge, ALU.mult).then_inc(gate_steps, 1)
            dve.tensor_scalar(gate_abs[:, :, :], rows, GATE_MIN, None, ALU.max).then_inc(gate_steps, 1)
            dve.tensor_scalar(gate_neg[:, :, :], rows, -1.0, GATE_MIN, ALU.mult, ALU.max).then_inc(gate_steps, 1)
            dve.wait_ge(gate_steps, 3)
            dve.tensor_tensor(gate_abs[:, :, :], gate_abs[:, :, :], gate_neg[:, :, :], ALU.max).then_inc(gate_steps, 1)
            dve.wait_ge(gate_steps, 4)
            dve.scalar_tensor_tensor(gate[:, :, :], gate_sign[:, :, :], -1.0, gate_abs[:, :, :], ALU.add,
                                     ALU.mult).then_inc(gate_steps, 1)
            dve.wait_ge(gate_steps, 5)
            dve.wait_ge(bout_in, 16)
            dve.tensor_tensor(boutg[:, :], bout_sb[:, :], gate[:, 1, :], ALU.mult).then_inc(gate_steps, 1)
            dve.wait_ge(gate_steps, 6)
            dve.tensor_copy(boutg_hi[:, :], boutg[:, :]).then_inc(gate_steps, 1)
            dve.wait_ge(gate_steps, 7)
            dve.tensor_tensor(boutg_lo[:, :], boutg[:, :], f(boutg_hi[:, :]), ALU.subtract).then_inc(gate_steps, 1)

            def set_up_ffn():
                dve.wait_ge(small_in, 11 * 16)
                dve.tensor_scalar(relu_bias[:, :], w1c[:, :], binc[:, 0:1], None, ALU.mult).then_inc(rbias, 1)
                dve.wait_ge(rbias, 1)
                dve.tensor_tensor(relu_bias[:, :], relu_bias[:, :], b1c[:, :], ALU.add).then_inc(rbias, 1)

            def step(i, live):
                if live(i - 2):
                    weigh(i - 2, 1)
                if live(i - 1):
                    row_max(i - 1, 0)
                    row_max(i - 1, 1)
                if live(i - 3):
                    accumulate(i - 3, 4)
                    accumulate(i - 3, 5)
                    accumulate(i - 3, 6)
                if live(i - 1):
                    low_v(i - 1, 0)
                    row_max(i - 1, 2)
                if live(i - 3):
                    accumulate(i - 3, 7)
                if live(i - 1):
                    low_v(i - 1, 1)
                    row_max(i - 1, 3)
                if live(i - 2):
                    statistics(1, i - 2)
                if live(i - 1):
                    recip(i - 1)
                    low_pt(i - 1, 0)
                    low_pt(i - 1, 1)
                if live(i + 1):
                    statistics(0, i + 1)
                if live(i):
                    low_h(i, 0)
                    low_h(i, 1)
                if live(i - 1):
                    low_pt(i - 1, 2)
                    weigh(i - 1, 0)
                if live(i):
                    low_t(i, 0)
                if live(i - 2):
                    accumulate(i - 2, 1)
                if live(i):
                    low_t(i, 1)
                if live(i - 2):
                    accumulate(i - 2, 2)
                    accumulate(i - 2, 3)

            set_up_ffn()
            steps(lambda i, live: step(i, live) if i >= 0 else None)


_IN = ["L0_attn_x", "L0_attn_WQ", "L0_attn_WK", "L0_attn_WV", "L0_ffn_Win", "L0_ffn_bin_", "L0_ffn_W1",
       "L0_ffn_b1", "L0_ffn_W2", "L0_ffn_b2", "L0_ffn_Wout", "L0_ffn_bout", "L0_c", "L0_wmod"]


def kernel(**inputs):
    import numpy as np
    import concourse.bacc as bacc
    from concourse.bass_utils import run_bass_kernel_spmd

    nc = bacc.Bacc("TRN2", target_bir_lowering=False, num_devices=1)
    arrays, args = {}, []
    for name in _IN:
        a = np.ascontiguousarray(inputs[name])
        arrays[name] = a
        args.append(nc.dram_tensor(name, a.shape, mybir.dt.from_np(a.dtype), kind="ExternalInput").ap())
    out = nc.dram_tensor("out", arrays["L0_attn_x"].shape, mybir.dt.float32, kind="ExternalOutput").ap()
    adaln_layer(nc, *args, out)
    return run_bass_kernel_spmd(nc, [arrays], core_ids=[0]).results[0]["out"]
```

```python
import concourse.bass as bass
from concourse import mybir
from contextlib import ExitStack


def adaln_layer(nc, x, WQ, WK, WV, Win, bin_, W1, b1, W2, b2, Wout, bout, c, wmod, out):
    fp32, fp32r, bf16 = mybir.dt.float32, mybir.dt.float32r, mybir.dt.bfloat16
    ALU, ACT, AX = mybir.AluOpType, mybir.ActivationFunctionType, mybir.AxisListType

    B, S, D = x.shape
    P = 128
    NT = S // P
    KD = D // P
    M, INNER = W1.shape
    NJ = INNER // 2
    HALF = NT // 2
    SCALE = float(D) ** -0.5
    EPS = 1e-5
    GATE_MIN = 0.25
    MASKED = -1.0e38
    SA, CA, GA, SB, CB, GB = range(6)
    MIN_N = 256

    ctx = ExitStack()
    with ctx:
        def sb(name, shape, dt=fp32):
            return ctx.enter_context(nc.sbuf_tensor(name, shape, dt))

        def sem(name):
            return ctx.enter_context(nc.semaphore(name))

        def f(ap):
            return ap.bitcast(fp32)

        ident = sb("ident", [P, P])
        ident_bf = sb("ident_bf", [P, P], bf16)
        mask_bf = sb("mask_bf", [P, P], bf16)
        minus_half = sb("minus_half", [P, NT])
        ones2 = sb("ones2", [2, P], fp32r)
        wq = sb("wq", [P, KD, D])
        wk = sb("wk", [P, KD, D])
        wqT = sb("wqT", [P, KD, D])
        wkT = sb("wkT", [P, KD, D])
        m_hi = sb("m_hi", [P, KD, D], fp32r)
        m_lo = sb("m_lo", [P, KD, D], fp32r)
        wv = sb("wv", [P, KD, D])
        wv_hi = sb("wv_hi", [P, KD, D], fp32r)
        wv_lo = sb("wv_lo", [P, KD, D], fp32r)
        win = sb("win", [P, KD, 2, M])
        wout = sb("wout", [P, D])
        w1c = sb("w1c", [P, NJ])
        b1c = sb("b1c", [P, NJ])
        w2c = sb("w2c", [P, NJ])
        b2c = sb("b2c", [P, 1])
        binc = sb("binc", [P, 1])
        relu_bias = sb("relu_bias", [P, NJ])
        c_sb = sb("c_sb", [B, D])
        cT = sb("cT", [P, KD * B])
        cT_exp = sb("cT_exp", [P, KD * B])
        cT_den = sb("cT_den", [P, KD * B])
        cT_sig = sb("cT_sig", [P, KD * B])
        siluT = sb("siluT", [P, KD, B])
        wmod_sb = sb("wmod_sb", [P, KD, 6, D])
        mod = sb("mod", [P, 4, KD, B])
        gateT_sign = sb("gateT_sign", [P, 2 * KD * B])
        gateT_pos = sb("gateT_pos", [P, 2 * KD * B])
        gateT_neg = sb("gateT_neg", [P, 2 * KD * B])
        gateT_abs = sb("gateT_abs", [P, 2 * KD * B])
        gateT = sb("gateT", [P, 2 * KD * B])
        gate = sb("gate", [B, 2, D])
        bout_sb = sb("bout_sb", [B, D])
        boutg = sb("boutg", [B, D])
        boutg_hi = sb("boutg_hi", [B, D], fp32r)
        boutg_lo = sb("boutg_lo", [B, D], fp32r)
        gates = sb("gates", [P, B, 2, D])
        bout2 = sb("bout2", [2, B, D], fp32r)
        xs = sb("xs", [P, B, NT, D])
        stat = [sb(f"stat{n}", [P, NT, 6]) for n in (1, 2)]
        mv = [sb(f"mv{n}", [P, NT, 2]) for n in (1, 2)]
        veps = [sb(f"veps{n}", [P, NT]) for n in (1, 2)]
        rstd = [sb(f"rstd{n}", [P, NT]) for n in (1, 2)]
        negmean = [sb(f"negmean{n}", [P, NT]) for n in (1, 2)]
        xn = [sb(f"xn{n}", [P, NT, D]) for n in (1, 2)]
        h_full = [sb(f"h_full{n}", [P, KD, S]) for n in (1, 2)]
        h_hi = sb("h_hi", [P, KD, S], fp32r)
        h_lo = sb("h_lo", [P, KD, S], fp32r)
        t_hi = sb("t_hi", [P, KD, S], fp32r)
        t_lo = sb("t_lo", [P, KD, S], fp32r)
        v_hi = sb("v_hi", [P, NT, D], fp32r)
        v_lo = sb("v_lo", [P, NT, D], fp32r)
        negmax = sb("negmax", [P, NT])
        den = sb("den", [P, NT])
        rden = sb("rden", [P, NT])
        probs = [sb(f"probs{i}", [P, (i + 1) * P]) for i in range(NT)]
        GROUPS = [[0, 1], [2], [3]]
        pt_hi = [sb(f"pt_hi{g}", [P, sum(i + 1 for i in q), P], fp32r) for g, q in enumerate(GROUPS)]
        pt_lo = [sb(f"pt_lo{g}", [P, sum(i + 1 for i in q), P], fp32r) for g, q in enumerate(GROUPS)]
        NG = len(GROUPS)
        y = sb("y", [P, NT, D])
        ffn = sb("ffn", [P, NT, D])
        relu = [sb(f"relu{k}", [P, S]) for k in range(NJ)]
        acc = [sb(f"acc{n}", [P, S]) for n in range(2)]
        wog = [sb(f"wog{n}", [P, D]) for n in range(2)]

        def pt_slot(i, j):
            g = next(n for n, q in enumerate(GROUPS) if i in q)
            return g, sum(k + 1 for k in GROUPS[g] if k < i) + j

        def bank(name):
            return ctx.enter_context(nc.psum_tensor(name, [P, S], fp32))

        A = [bank("A0"), bank("A1")]
        SC = [bank("B0"), bank("B1")]
        C = [bank("C0"), bank("C1")]
        E = [bank("D0"), bank("D1")]

        gate_dram = nc.dram_tensor("gate_scratch", [B, 2 * D], fp32)
        bout_dram = nc.dram_tensor("bout_scratch", [2, B, D], fp32)

        c_in, wmod_in, wmod2_in = sem("c_in"), sem("wmod_in"), sem("wmod2_in")
        wqk_in, wv_in, win_in, small_in, bout_in = sem("wqk_in"), sem("wv_in"), sem("win_in"), sem("small_in"), sem("bout_in")
        consts, b2_zero = sem("consts"), sem("b2_zero")
        cT_pe, cT_sb, c_exped, c_steps, siluT_sb = sem("cT_pe"), sem("cT_sb"), sem("c_exped"), sem("c_steps"), sem("siluT_sb")
        wT_pe, wT_sb, m_pe, m_hi_sb, m_lo_sb = sem("wT_pe"), sem("wT_sb"), sem("m_pe"), sem("m_hi_sb"), sem("m_lo_sb")
        w_hi_sb, w_lo_sb = sem("w_hi_sb"), sem("w_lo_sb")
        mod_pe, mod_sb, gate_pe, gate_steps = sem("mod_pe"), sem("mod_sb"), sem("gate_pe"), sem("gate_steps")
        gate_rows, bout_steps = sem("gate_rows"), sem("bout_steps")
        gate_out, bout_out, gates_in, bout2_in = sem("gate_out"), sem("bout_out"), sem("gates_in"), sem("bout2_in")
        rbias = sem("rbias")
        x_in = sem("x_in")
        stat_d = [sem(f"stat_d{n}") for n in (1, 2)]
        aggr_d = [sem(f"aggr_d{n}") for n in (1, 2)]
        veps_d = [sem(f"veps_d{n}") for n in (1, 2)]
        rstd_p = [sem(f"rstd_p{n}") for n in (1, 2)]
        negmean_d = [sem(f"negmean_d{n}") for n in (1, 2)]
        xn_p = [sem(f"xn_p{n}") for n in (1, 2)]
        xT_pe = [sem(f"xT_pe{n}") for n in (1, 2)]
        h_full_a = [sem(f"h_full_a{n}") for n in (1, 2)]
        h_hi_a, h_lo_made = sem("h_hi_a"), sem("h_lo_made")
        t_pe, t_hi_a, t_lo_d = sem("t_pe"), sem("t_hi_a"), sem("t_lo_d")
        v_pe, v_hi_a, v_lo_d = sem("v_pe"), sem("v_hi_a"), sem("v_lo_d")
        sc_pe, max_d, exp_a = sem("sc_pe"), sem("max_d"), sem("exp_a")
        pt_pe, pt_hi_a, pt_lo_d = sem("pt_pe"), sem("pt_hi_a"), sem("pt_lo_d")
        rden_d, pv_pe, y_d, x2_p = sem("rden_d"), sem("pv_pe"), sem("y_d"), sem("x2_p")
        s_pe, relu_a, acc_d = sem("s_pe"), sem("relu_a"), sem("acc_d")
        wog_p = sem("wog_p")
        o_pe, ffn_a, fin_p, stored = sem("o_pe"), sem("ffn_a"), sem("fin_p"), sem("stored")

        end_stat, end_aggr, end_var = sem("end_stat"), sem("end_aggr"), sem("end_var")
        end_rstd, end_xn, end_xT = sem("end_rstd"), sem("end_xn"), sem("end_xT")
        end_h, end_s, end_relu = sem("end_h"), sem("end_s"), sem("end_relu")
        end_acc = [sem(f"end_acc{h}") for h in range(2)]
        end_o, end_fin, end_stored = sem("end_o"), sem("end_fin"), sem("end_stored")

        block = ctx.enter_context(nc.Block())

        def expand_bank(b, k):
            return (A if b == B - 2 else E)[k]

        def output_bank(b, h):
            return SC[h] if b < B - 3 else expand_bank(b, 1 - h)

        def steps(step):
            for i in range(-1, B):
                step(i, lambda b: 0 <= b < B)

        @block.sync
        def _(sp):
            x_v = x.rearrange("b (i p) d -> p b i d", p=P)
            out_v = out.rearrange("b (i p) d -> p b i d", p=P)

            def load(b):
                sp.dma_start(xs[:, b, :, :], x_v[:, b, :, :]).then_inc(x_in, 16)

            def store(b, h):
                sp.wait_ge(fin_p, 2 * b + h + 1)
                sp.dma_start(out_v[:, b, HALF * h:HALF * (h + 1), :],
                             xs[:, b, HALF * h:HALF * (h + 1), :]).then_inc(stored, 16)

            load(0)
            sp.dma_start(wq[:, :, :], WQ.rearrange("(k p) e -> p k e", p=P)).then_inc(wqk_in, 16)
            sp.dma_start(wk[:, :, :], WK.rearrange("(k p) e -> p k e", p=P)).then_inc(wqk_in, 16)
            sp.dma_start(wv[:, :, :], WV.rearrange("(k p) e -> p k e", p=P)).then_inc(wv_in, 16)
            for r in range(2):
                sp.dma_start(win[:, :, r, :], Win.rearrange("(k p) m -> p k m", p=P)).then_inc(win_in, 16)
            sp.wait_ge(x_in, 16)
            load(1)
            sp.wait_ge(b2_zero, 1)
            for r in range(2):
                q = slice(r * M, (r + 1) * M)
                sp.dma_start(w1c[q, :], W1[:, r * NJ:(r + 1) * NJ]).then_inc(small_in, 16)
                sp.dma_start(b1c[q, :], b1[:, r * NJ:(r + 1) * NJ]).then_inc(small_in, 16)
                sp.dma_start(w2c[q, :], W2[:, r * NJ:(r + 1) * NJ]).then_inc(small_in, 16)
                sp.dma_start(binc[q, :], bin_.rearrange("(m a) -> m a", a=1)).then_inc(small_in, 16)
                sp.dma_start(wout[q, :], Wout[:, :]).then_inc(small_in, 16)
            sp.dma_start(b2c[0:M, :], b2.rearrange("(m a) -> m a", a=1)).then_inc(small_in, 16)
            sp.wait_ge(x_in, 32)
            load(2)
            sp.wait_ge(gate_rows, 1)
            sp.dma_start(gate_dram[:, :], gate[:, :, :].rearrange("b n d -> b (n d)")).then_inc(gate_out, 16)
            sp.wait_ge(gate_out, 16)
            sp.dma_start(gates[:, :, :, :].rearrange("p b n d -> p (b n d)"),
                         gate_dram[:, :].rearrange("b n -> (b n)").partition_broadcast(P)).then_inc(gates_in, 16)
            sp.wait_ge(bout_steps, 3)
            sp.dma_start(bout_dram[0, :, :], f(boutg_hi[:, :])).then_inc(bout_out, 16)
            sp.dma_start(bout_dram[1, :, :], f(boutg_lo[:, :])).then_inc(bout_out, 16)
            sp.wait_ge(bout_out, 32)
            sp.dma_start(f(bout2[:, :, :]), bout_dram[:, :, :]).then_inc(bout2_in, 16)

            def step(i, live):
                if live(i + 3):
                    sp.wait_ge(x_in, 16 * (i + 3))
                    load(i + 3)
                if live(i - 3):
                    store(i - 3, 0)
                    store(i - 3, 1)

            steps(lambda i, live: step(i, live) if i >= 0 else None)
            for b in (B - 3, B - 2):
                store(b, 0)
                store(b, 1)
            for i in range(NT):
                sp.wait_ge(end_fin, i + 1)
                sp.dma_start(out_v[:, B - 1, i, :], xs[:, B - 1, i, :]).then_inc(end_stored, 16)
            sp.wait_ge(stored, 2 * (B - 1) * 16)
            sp.wait_ge(end_stored, NT * 16)

        @block.gpsimd
        def _(pool):
            pool.memset(b2c[:, :], 0.0).then_inc(b2_zero, 1)
            pool.memset(ident[:, :], 0.0).then_inc(consts, 1)
            pool.memset(mask_bf[:, :], 0.0).then_inc(consts, 1)
            pool.memset(minus_half[:, :], -0.5).then_inc(consts, 1)
            pool.memset(f(ones2[:, :]), 1.0).then_inc(consts, 1)
            pool.memset(ident_bf[:, :], 0.0).then_inc(consts, 1)
            pool.wait_ge(consts, 5)
            for m in (ident, ident_bf):
                pool.affine_select(out=m[:, :], in_=m[:, :], compare_op=ALU.not_equal, fill=1.0, base=0,
                                   pattern=[[-1, P]], channel_multiplier=1).then_inc(consts, 1)
            pool.affine_select(out=mask_bf[:, :], in_=mask_bf[:, :], compare_op=ALU.is_ge, fill=MASKED, base=0,
                               pattern=[[-1, P]], channel_multiplier=1).then_inc(consts, 1)

            def rsqrt(n, b):
                pool.wait_ge(veps_d[n], b + 1)
                if b > 0:
                    pool.wait_ge(xn_p[n], NT * b)
                pool.tensor_tensor(rstd[n][:, :], veps[n][:, :], minus_half[:, :], ALU.pow).then_inc(rstd_p[n], 1)

            def normalise(n, b):
                pool.wait_ge(negmean_d[n], b + 1)
                pool.wait_ge(rstd_p[n], b + 1)
                if b > 0:
                    pool.wait_ge(xT_pe[n], KD * b)
                for i in range(NT):
                    pool.tensor_scalar(xn[n][:, i, :], xs[:, b, i, :], negmean[n][:, i:i + 1], rstd[n][:, i:i + 1],
                                       ALU.add, ALU.mult).then_inc(xn_p[n], 1)

            def gate_wout(b):
                if b == 0:
                    pool.wait_ge(small_in, 11 * 16)
                    pool.wait_ge(gates_in, 16)
                if b >= 2:
                    pool.wait_ge(o_pe, 2 * (b - 1))
                pool.tensor_tensor(wog[b % 2][:, :], wout[:, :], gates[:, b, 1, :], ALU.mult).then_inc(wog_p, 1)

            def low_h(b, k):
                pool.wait_ge(h_hi_a, KD * b + k + 1)
                pool.tensor_tensor(h_lo[:, k, :], h_full[0][:, k, :], f(h_hi[:, k, :]),
                                   ALU.subtract).then_inc(h_lo_made, 1)

            def add_attention(b, h):
                pool.wait_ge(y_d, NT * b + HALF * (h + 1))
                q = slice(HALF * h, HALF * (h + 1))
                pool.tensor_tensor(xs[:, b, q, :], xs[:, b, q, :], y[:, q, :], ALU.add).then_inc(x2_p, 1)

            def finish(b, h):
                pool.wait_ge(ffn_a, 2 * b + h + 1)
                q = slice(HALF * h, HALF * (h + 1))
                pool.tensor_tensor(xs[:, b, q, :], xs[:, b, q, :], ffn[:, q, :], ALU.add).then_inc(fin_p, 1)

            def start_sum(b):
                if b == 0:
                    pool.wait_ge(small_in, 11 * 16)
                pool.wait_ge(relu_a, NJ * b + 1)
                if b >= 2:
                    pool.wait_ge(o_pe, 2 * (b - 1))
                pool.tensor_scalar(acc[b % 2][:, :], relu[0][:, :], w2c[:, 0:1], b2c[:, 0:1], ALU.mult,
                                   ALU.add).then_inc(acc_d, 1)

            def step(i, live):
                if live(i - 2):
                    add_attention(i - 2, 1)
                    rsqrt(1, i - 2)
                    normalise(1, i - 2)
                if live(i - 3):
                    gate_wout(i - 3)
                if live(i):
                    low_h(i, 0)
                if live(i - 1):
                    add_attention(i - 1, 0)
                if live(i - 2):
                    start_sum(i - 2)
                if live(i - 3):
                    finish(i - 3, 0)
                if live(i + 1):
                    rsqrt(0, i + 1)
                if live(i - 3):
                    finish(i - 3, 1)
                if live(i + 1):
                    normalise(0, i + 1)

            steps(step)

            def end_normalise(h):
                pool.wait_ge(end_var, 2 * (h + 1))
                q = slice(HALF * h, HALF * (h + 1))
                if h == 0:
                    pool.wait_ge(xn_p[1], NT * (B - 1))
                pool.tensor_tensor(rstd[1][:, q], veps[1][:, q], minus_half[:, q], ALU.pow).then_inc(end_rstd, 1)
                pool.wait_ge(end_rstd, h + 1)
                if h == 0:
                    pool.wait_ge(xT_pe[1], KD * (B - 1))
                for i in range(HALF * h, HALF * (h + 1)):
                    pool.tensor_scalar(xn[1][:, i, :], xs[:, B - 1, i, :], negmean[1][:, i:i + 1], rstd[1][:, i:i + 1],
                                       ALU.add, ALU.mult).then_inc(end_xn, 1)

            def end_start_sum(h):
                pool.wait_ge(end_relu, NJ * h + 1)
                if h == 0:
                    pool.wait_ge(o_pe, 2 * (B - 2))
                q = slice(HALF * P * h, HALF * P * (h + 1))
                pool.tensor_scalar(acc[(B - 1) % 2][:, q], relu[0][:, q], w2c[:, 0:1], b2c[:, 0:1], ALU.mult,
                                   ALU.add).then_inc(end_acc[h], 1)

            gate_wout(B - 3)
            add_attention(B - 2, 1)
            rsqrt(1, B - 2)
            normalise(1, B - 2)
            add_attention(B - 1, 0)
            start_sum(B - 2)
            end_normalise(0)
            add_attention(B - 1, 1)
            end_normalise(1)
            end_start_sum(0)
            gate_wout(B - 2)
            gate_wout(B - 1)
            finish(B - 3, 0)
            finish(B - 3, 1)
            end_start_sum(1)
            finish(B - 2, 0)
            finish(B - 2, 1)

        @block.scalar
        def _(act):
            act.dma_start(c_sb[:, :], c).then_inc(c_in, 16)
            wm = wmod.rearrange("(k p) (q d) -> p k q d", p=P, d=D)
            act.dma_start(wmod_sb[:, :, SA:CA + 1, :], wm[:, :, SA:CA + 1, :]).then_inc(wmod_in, 16)
            act.dma_start(wmod_sb[:, :, GA:GB + 1, :], wm[:, :, GA:GB + 1, :]).then_inc(wmod2_in, 16)
            act.dma_start(bout_sb[:, :], bout.partition_broadcast(B)).then_inc(bout_in, 16)
            act.wait_ge(cT_sb, 1)
            act.activation(cT_exp[:, :], cT[:, :], ACT.Exp, scale=-1.0).then_inc(c_exped, 1)
            for n, dst in enumerate((wqT, wkT)):
                act.wait_ge(wT_pe, n + 1)
                act.activation(dst[:, :, :], SC[n][:, :].rearrange("p (k d) -> p k d", k=KD), ACT.Copy).then_inc(wT_sb, 1)

            def round_m(k):
                act.wait_ge(m_pe, k + 1)
                act.activation(m_hi[:, k, :], C[k][:, 0:D], ACT.Copy, scale=SCALE).then_inc(m_hi_sb, 1)

            def modulate(n, b, k):
                act.wait_ge(xT_pe[n], KD * b + k + 1)
                if n == 0 and b == 0 and k == 0:
                    act.wait_ge(mod_sb, 1)
                if n == 1 and b == 0 and k == 0:
                    act.wait_ge(mod_sb, 2)
                if b > 0 and k == 0:
                    act.wait_ge(h_lo_made if n == 0 else s_pe, (KD if n == 0 else 1) * b)
                act.activation(h_full[n][:, k, :], (A[k] if n == 0 else expand_bank(b, k))[:, :], ACT.Identity,
                               bias=mod[:, 2 * n, k, b:b + 1],
                               scale=mod[:, 2 * n + 1, k, b:b + 1]).then_inc(h_full_a[n], 1)

            def round_h(b, k):
                if k == 0 and b > 0:
                    act.wait_ge(sc_pe, NT * b)
                    act.wait_ge(v_pe, 2 * b)
                act.wait_ge(h_full_a[0], KD * b + k + 1)
                act.activation(h_hi[:, k, :], h_full[0][:, k, :], ACT.Copy).then_inc(h_hi_a, 1)

            def exps(b, i):
                act.wait_ge(max_d, NT * b + i + 1)
                if b > 0:
                    act.wait_ge(pt_pe, NG * b)
                    act.wait_ge(rden_d, b)
                act.activation(probs[i][:, :], SC[i % 2][:, 0:(i + 1) * P], ACT.Exp, bias=negmax[:, i:i + 1],
                               accum_out=den[:, i:i + 1]).then_inc(exp_a, 1)

            def round_pt(b, g):
                n = pt_hi[g].shape[1]
                act.wait_ge(pt_pe, NG * b + g + 1)
                if b > 0:
                    act.wait_ge(pv_pe, 2 * b)
                act.activation(pt_hi[g][:, :, :], C[g % 2][:, 0:n * P].rearrange("p (n q) -> p n q", q=P),
                               ACT.Copy).then_inc(pt_hi_a, 1)

            def round_t(b, m):
                act.wait_ge(t_pe, KD * b + m + 1)
                if b > 0:
                    act.wait_ge(sc_pe, NT * b)
                act.activation(t_hi[:, m, :], A[m][:, :], ACT.Copy).then_inc(t_hi_a, 1)

            def round_v(b, h):
                act.wait_ge(v_pe, 2 * b + h + 1)
                if b > 0:
                    act.wait_ge(pv_pe, 2 * b)
                act.activation(v_hi[:, HALF * h:HALF * (h + 1), :], A[h][:, :].rearrange("p (i d) -> p i d", d=D),
                               ACT.Copy).then_inc(v_hi_a, 1)

            def copy_ffn(b, h):
                act.wait_ge(o_pe, 2 * b + h + 1)
                if b > 0:
                    act.wait_ge(fin_p, 2 * (b - 1) + h + 1)
                act.activation(ffn[:, HALF * h:HALF * (h + 1), :], output_bank(b, h)[:, :].rearrange("p (i d) -> p i d", d=D),
                               ACT.Copy).then_inc(ffn_a, 1)

            def relus(b, j):
                if j == 0:
                    act.wait_ge(s_pe, b + 1)
                    if b == 0:
                        act.wait_ge(rbias, 2)
                if b > 0:
                    act.wait_ge(acc_d, NJ * (b - 1) + j + 1)
                act.activation(relu[j][:, :], expand_bank(b, 0)[:, :], ACT.Relu, bias=relu_bias[:, j:j + 1],
                               scale=w1c[:, j:j + 1]).then_inc(relu_a, 1)

            def step(i, live):
                if live(i - 3):
                    relus(i - 3, 4)
                    relus(i - 3, 5)
                    relus(i - 3, 6)
                    relus(i - 3, 7)
                if live(i - 1):
                    round_v(i - 1, 0)
                    exps(i - 1, 0)
                    exps(i - 1, 1)
                    round_v(i - 1, 1)
                    exps(i - 1, 2)
                    round_pt(i - 1, 0)
                    round_pt(i - 1, 1)
                    exps(i - 1, 3)
                if live(i):
                    modulate(0, i, 0)
                    modulate(0, i, 1)
                    round_h(i, 0)
                if i == 0:
                    round_m(0)
                if live(i):
                    round_h(i, 1)
                if live(i - 1):
                    round_pt(i - 1, 2)
                if live(i - 2):
                    modulate(1, i - 2, 0)
                    modulate(1, i - 2, 1)
                if i == 0:
                    round_m(1)
                if live(i - 3):
                    copy_ffn(i - 3, 0)
                if live(i):
                    round_t(i, 0)
                if live(i - 2):
                    relus(i - 2, 0)
                    relus(i - 2, 1)
                if live(i):
                    round_t(i, 1)
                if live(i - 2):
                    relus(i - 2, 2)
                    relus(i - 2, 3)
                if live(i - 3):
                    copy_ffn(i - 3, 1)

            steps(step)

            def end_modulate(h):
                act.wait_ge(end_xT, h + 1)
                if h == 0:
                    act.wait_ge(s_pe, B - 1)
                for k in range(KD):
                    act.activation(h_full[1][:, k, HALF * P * h:HALF * P * (h + 1)],
                                   C[1 - h][:, k * HALF * P:(k + 1) * HALF * P], ACT.Identity,
                                   bias=mod[:, 2, k, B - 1:B], scale=mod[:, 3, k, B - 1:B]).then_inc(end_h, 1)

            def end_relus(h, j):
                act.wait_ge(end_s, h + 1)
                q = slice(HALF * P * h, HALF * P * (h + 1))
                if h == 0:
                    act.wait_ge(acc_d, NJ * (B - 2) + j + 1)
                act.activation(relu[j][:, q], SC[h][:, 0:HALF * P], ACT.Relu, bias=relu_bias[:, j:j + 1],
                               scale=w1c[:, j:j + 1]).then_inc(end_relu, 1)

            for j in range(4, 6):
                relus(B - 3, j)
            exps(B - 1, 0)
            relus(B - 3, 6)
            round_v(B - 1, 0)
            exps(B - 1, 1)
            exps(B - 1, 2)
            round_v(B - 1, 1)
            round_pt(B - 1, 0)
            exps(B - 1, 3)
            round_pt(B - 1, 1)
            relus(B - 3, 7)
            modulate(1, B - 2, 0)
            modulate(1, B - 2, 1)
            round_pt(B - 1, 2)
            for j in range(0, 7):
                relus(B - 2, j)
            end_modulate(0)
            copy_ffn(B - 3, 0)
            relus(B - 2, 7)
            for j in range(0, 5):
                end_relus(0, j)
            end_modulate(1)
            copy_ffn(B - 3, 1)
            for j in range(5, NJ):
                end_relus(0, j)
            for j in range(0, 5):
                end_relus(1, j)
            copy_ffn(B - 2, 0)
            copy_ffn(B - 2, 1)
            for j in range(5, NJ):
                end_relus(1, j)

        @block.tensor
        def _(pe):
            def three(dst, lhs, rhs, parts, more=False):
                n = len(parts)
                for q, part in enumerate(parts):
                    lh, ll, rh, rl = lhs[0](part), lhs[1](part), rhs[0](part), rhs[1](part)
                    pe.matmul(dst, ll, rh, start=(q == 0), stop=False)
                    pe.matmul(dst, lh, rl, start=False, stop=False)
                    mm = pe.matmul(dst, lh, rh, start=False, stop=(q == n - 1 and not more))
                return mm

            def keep_busy(count):
                for _ in range(count):
                    pe.transpose(SC[1][:, 0:P], ident[:, :], ident[:, :])

            pe.wait_ge(consts, 8)
            keep_busy(8)
            pe.wait_ge(c_in, 16)
            for k in range(KD):
                mm = pe.transpose(E[0][:, k * B:(k + 1) * B], c_sb[:, k * P:(k + 1) * P], ident[0:B, 0:B])
            mm.then_inc(cT_pe, 1)
            keep_busy(12)
            pe.wait_ge(wqk_in, 32)
            for n, w in enumerate((wq, wk)):
                for e in range(KD):
                    for d in range(KD):
                        mm = pe.transpose(SC[n][:, e * D + d * P:e * D + (d + 1) * P],
                                          w[:, d, e * P:(e + 1) * P], ident[:, :])
                mm.then_inc(wT_pe, 1)

            def make_m(d):
                pe.wait_ge(wT_sb, 2)
                for e in range(KD):
                    mm = pe.matmul(C[d][:, 0:D], wqT[:, e, d * P:(d + 1) * P], wkT[:, e, :],
                                   start=(e == 0), stop=(e == KD - 1))
                mm.then_inc(m_pe, 1)

            def modulation(n, qs):
                if n == 1:
                    pe.wait_ge(wmod2_in, 16)
                    pe.wait_ge(mod_sb, 1)
                if n == 2:
                    pe.wait_ge(gate_steps, 3)
                for q, which in enumerate(qs):
                    for k in range(KD):
                        for e in range(KD):
                            col = ((2 * n + q) * KD + k) * B
                            mm = pe.matmul(E[1][:, col:col + B], wmod_sb[:, e, which, k * P:(k + 1) * P],
                                           siluT[:, e, :], start=(e == 0), stop=(e == KD - 1))
                mm.then_inc(mod_pe, 1)

            def transpose_x(n, b, k):
                pe.wait_ge(xn_p[n], NT * (b + 1))
                dst = A[k] if n == 0 else expand_bank(b, k)
                if n == 0 and b > 0:
                    pe.wait_ge(v_lo_d, 2 * (b - 1) + k + 1)
                if n == 1:
                    if b == 0:
                        pe.wait_ge(mod_sb, 2)
                    if b == B - 2:
                        pe.wait_ge(v_lo_d, 2 * B)
                    elif b > 0:
                        pe.wait_ge(relu_a, NJ * b)
                for i in range(NT):
                    mm = pe.transpose(dst[:, i * P:(i + 1) * P], xn[n][:, i, k * P:(k + 1) * P], ident[:, :])
                mm.then_inc(xT_pe[n], 1)

            def project_t(b, m):
                if b == 0:
                    pe.wait_ge(m_lo_sb, KD)
                pe.wait_ge(h_lo_made, KD * (b + 1))
                three(A[m][:, :],
                      [lambda k, w=w: w[:, k, m * P:(m + 1) * P] for w in (m_hi, m_lo)],
                      [lambda k, w=w: w[:, k, :] for w in (h_hi, h_lo)], range(KD)).then_inc(t_pe, 1)

            def project_v(b, h):
                if b == 0:
                    pe.wait_ge(w_lo_sb, 1)
                pe.wait_ge(t_lo_d, KD * b + h + 1)
                for n in range(HALF):
                    i = HALF * h + n
                    mm = three(A[h][:, n * D:(n + 1) * D],
                               [lambda k, w=w, i=i: w[:, k, i * P:(i + 1) * P] for w in (h_hi, h_lo)],
                               [lambda k, w=w: w[:, k, :] for w in (wv_hi, wv_lo)], range(KD))
                mm.then_inc(v_pe, 1)

            def scores(b, i):
                if i == 0:
                    pe.wait_ge(t_lo_d, KD * (b + 1))
                if b > 0 or i >= 2:
                    pe.wait_ge(exp_a, NT * b + i - 1)
                if b >= 3 and i < 2:
                    pe.wait_ge(ffn_a, 2 * (b - 3) + i + 1)
                width = max((i + 1) * P, MIN_N)
                dst = SC[i % 2]
                three(dst[:, 0:width],
                      [lambda k, w=w: w[:, k, i * P:(i + 1) * P] for w in (t_hi, t_lo)],
                      [lambda k, w=w: w[:, k, 0:width] for w in (h_hi, h_lo)], range(KD), more=True)
                pe.matmul(dst[:, i * P:(i + 1) * P], ident_bf[:, :], mask_bf[:, :], start=False,
                          stop=True).then_inc(sc_pe, 1)

            def transpose_p(b, g):
                pe.wait_ge(exp_a, NT * b + GROUPS[g][-1] + 1)
                if g < 2:
                    if b > 0:
                        pe.wait_ge(y_d, NT * b)
                    else:
                        pe.wait_ge(gate_rows, 1)
                else:
                    pe.wait_ge(pt_lo_d, NG * b + 1)
                for i in GROUPS[g]:
                    for j in range(i + 1):
                        s = pt_slot(i, j)[1]
                        mm = pe.transpose(C[g % 2][:, s * P:(s + 1) * P], probs[i][:, j * P:(j + 1) * P], ident[:, :])
                mm.then_inc(pt_pe, 1)

            def attend(b, h):
                pe.wait_ge(pt_lo_d, NG * b + 2 + h)
                pe.wait_ge(v_lo_d, 2 * b + 1 + h)
                for n in range(HALF):
                    i = HALF * h + n
                    g = pt_slot(i, 0)[0]
                    mm = three(C[1 - h][:, n * D:(n + 1) * D],
                               [lambda j, w=w: w[g][:, pt_slot(i, j)[1], :] for w in (pt_hi, pt_lo)],
                               [lambda j, w=w: w[:, j, :] for w in (v_hi, v_lo)], range(i + 1))
                mm.then_inc(pv_pe, 1)

            def hidden(b):
                if b == 0:
                    pe.wait_ge(win_in, 32)
                pe.wait_ge(h_full_a[1], KD * (b + 1))
                for k in range(KD):
                    mm = pe.matmul(expand_bank(b, 0)[:, :], win[:, k, :, :].rearrange("p r m -> p (r m)"), h_full[1][:, k, :],
                                   start=(k == 0), stop=(k == KD - 1))
                mm.then_inc(s_pe, 1)

            def output(b, h):
                if h == 0:
                    pe.wait_ge(acc_d, NJ * (b + 1))
                    pe.wait_ge(wog_p, b + 1)
                    if b == 0:
                        pe.wait_ge(bout2_in, 16)
                if b < B - 3:
                    pe.wait_ge(exp_a, NT * (b + 3))
                for n in range(HALF):
                    i = HALF * h + n
                    dst = output_bank(b, h)[:, n * D:(n + 1) * D]
                    pe.matmul(dst, acc[b % 2][:, i * P:(i + 1) * P], wog[b % 2][:, :], start=True, stop=False)
                    mm = pe.matmul(dst, ones2[:, :], bout2[:, b, :], start=False, stop=True)
                mm.then_inc(o_pe, 1)

            def transpose_gates():
                pe.wait_ge(m_lo_sb, KD)
                pe.wait_ge(gate_steps, 5)
                for n in range(2):
                    for k in range(KD):
                        mm = pe.transpose(C[1][0:B, n * D + k * P:n * D + (k + 1) * P],
                                          gateT[:, (n * KD + k) * B:(n * KD + k + 1) * B], ident[:, :])
                mm.then_inc(gate_pe, 1)

            def step(i, live):
                if live(i - 1):
                    scores(i - 1, 0)
                    scores(i - 1, 1)
                if live(i - 1) and i > 1:
                    project_v(i - 1, 0)
                if live(i - 1):
                    project_v(i - 1, 1)
                    scores(i - 1, 2)
                    transpose_p(i - 1, 0)
                    scores(i - 1, 3)
                    transpose_p(i - 1, 1)
                if live(i) and i > 0:
                    transpose_x(0, i, 0)
                    transpose_x(0, i, 1)
                if i == 1:
                    modulation(2, (SB, CB))
                if live(i - 1):
                    transpose_p(i - 1, 2)
                    attend(i - 1, 0)
                if live(i - 2):
                    transpose_x(1, i - 2, 0)
                if i == 0:
                    modulation(1, (GA, GB))
                if live(i - 3):
                    output(i - 3, 0)
                if live(i - 2):
                    transpose_x(1, i - 2, 1)
                if live(i):
                    project_t(i, 0)
                if live(i - 2):
                    hidden(i - 2)
                if live(i):
                    project_t(i, 1)
                if live(i - 3):
                    output(i - 3, 1)
                if live(i - 1):
                    attend(i - 1, 1)
                if i == 0:
                    project_v(0, 0)
                    transpose_gates()

            pe.wait_ge(siluT_sb, 1)
            pe.wait_ge(wmod_in, 16)
            modulation(0, (SA, CA))
            transpose_x(0, 0, 0)
            transpose_x(0, 0, 1)
            make_m(0)
            make_m(1)
            keep_busy(8)

            steps(lambda i, live: step(i, live) if i >= 0 else None)

            def end_transpose_x(h):
                pe.wait_ge(end_xn, HALF * (h + 1))
                pe.wait_ge(y_d, NT * (B - 1) + HALF * (h + 1))
                for k in range(KD):
                    for n in range(HALF):
                        at = (k * HALF + n) * P
                        mm = pe.transpose(C[1 - h][:, at:at + P], xn[1][:, HALF * h + n, k * P:(k + 1) * P], ident[:, :])
                mm.then_inc(end_xT, 1)

            def end_hidden(h):
                pe.wait_ge(exp_a, NT * B)
                pe.wait_ge(end_h, KD * (h + 1))
                for k in range(KD):
                    mm = pe.matmul(SC[h][:, 0:HALF * P], win[:, k, :, :].rearrange("p r m -> p (r m)"),
                                   h_full[1][:, k, HALF * P * h:HALF * P * (h + 1)], start=(k == 0), stop=(k == KD - 1))
                mm.then_inc(end_s, 1)

            def end_output(h):
                pe.wait_ge(end_acc[h], NJ)
                pe.wait_ge(wog_p, B)
                pe.wait_ge(ffn_a, 2 * (B - 2))
                for n in range(HALF):
                    i = HALF * h + n
                    dst = (E, C)[h][n][:, 0:D]
                    pe.matmul(dst, acc[(B - 1) % 2][:, i * P:(i + 1) * P], wog[(B - 1) % 2][:, :], start=True, stop=False)
                    pe.matmul(dst, ones2[:, :], bout2[:, B - 1, :], start=False, stop=True).then_inc(end_o, 1)

            scores(B - 1, 0)
            scores(B - 1, 1)
            project_v(B - 1, 0)
            scores(B - 1, 2)
            project_v(B - 1, 1)
            scores(B - 1, 3)
            transpose_p(B - 1, 0)
            transpose_p(B - 1, 1)
            transpose_p(B - 1, 2)
            transpose_x(1, B - 2, 0)
            transpose_x(1, B - 2, 1)
            attend(B - 1, 0)
            hidden(B - 2)
            attend(B - 1, 1)
            output(B - 3, 0)
            end_transpose_x(0)
            output(B - 3, 1)
            end_hidden(0)
            end_transpose_x(1)
            end_hidden(1)
            output(B - 2, 0)
            output(B - 2, 1)
            end_output(0)
            end_output(1)

        @block.vector
        def _(dve):
            def token_stats(n, b, h):
                if n == 0:
                    dve.wait_ge(x_in, 16 * (b + 1))
                else:
                    dve.wait_ge(x2_p, 2 * b + h + 1)
                if b > 0:
                    dve.wait_ge(aggr_d[n], NT * b)
                for i in range(HALF * h, HALF * (h + 1)):
                    dve.bn_stats(stat[n][:, i, :], xs[:, b, i, :]).then_inc(stat_d[n], 1)

            def aggregate(n, b):
                if b > 0:
                    dve.wait_ge(veps_d[n], b)
                    dve.wait_ge(negmean_d[n], b)
                for i in range(NT):
                    dve.wait_ge(stat_d[n], NT * b + i + 1)
                    dve.bn_aggr(mv[n][:, i, :], stat[n][:, i, :]).then_inc(aggr_d[n], 1)
                dve.wait_ge(aggr_d[n], NT * (b + 1))
                if b > 0:
                    dve.wait_ge(rstd_p[n], b)
                dve.tensor_scalar(veps[n][:, :], mv[n][:, :, 1], EPS, None, ALU.add).then_inc(veps_d[n], 1)
                if b > 0:
                    dve.wait_ge(xn_p[n], NT * b)
                dve.tensor_scalar(negmean[n][:, :], mv[n][:, :, 0], -1.0, None, ALU.mult).then_inc(negmean_d[n], 1)

            def statistics(n, b):
                token_stats(n, b, 0)
                token_stats(n, b, 1)
                aggregate(n, b)

            def low_h(b, k):
                dve.wait_ge(h_hi_a, KD * b + k + 1)
                dve.tensor_tensor(h_lo[:, k, :], h_full[0][:, k, :], f(h_hi[:, k, :]),
                                  ALU.subtract).then_inc(h_lo_made, 1)

            def low_t(b, m):
                dve.wait_ge(t_hi_a, KD * b + m + 1)
                dve.tensor_tensor(t_lo[:, m, :], A[m][:, :], f(t_hi[:, m, :]), ALU.subtract).then_inc(t_lo_d, 1)

            def low_v(b, h):
                dve.wait_ge(v_hi_a, 2 * b + h + 1)
                q = slice(HALF * h, HALF * (h + 1))
                dve.tensor_tensor(v_lo[:, q, :], A[h][:, :].rearrange("p (i d) -> p i d", d=D), f(v_hi[:, q, :]),
                                  ALU.subtract).then_inc(v_lo_d, 1)

            def row_max(b, i):
                dve.wait_ge(sc_pe, NT * b + i + 1)
                if b > 0:
                    dve.wait_ge(exp_a, NT * (b - 1) + i + 1)
                dve.tensor_reduce(negmax[:, i:i + 1], SC[i % 2][:, 0:(i + 1) * P], AX.X, ALU.max,
                                  negate=True).then_inc(max_d, 1)

            def low_pt(b, g):
                n = pt_hi[g].shape[1]
                dve.wait_ge(pt_hi_a, NG * b + g + 1)
                dve.tensor_tensor(pt_lo[g][:, :, :], C[g % 2][:, 0:n * P].rearrange("p (n q) -> p n q", q=P),
                                  f(pt_hi[g][:, :, :]), ALU.subtract).then_inc(pt_lo_d, 1)

            def recip(b):
                dve.wait_ge(exp_a, NT * (b + 1))
                if b > 0:
                    dve.wait_ge(y_d, NT * b)
                dve.reciprocal(rden[:, :], den[:, :]).then_inc(rden_d, 1)

            def weigh(b, h):
                if h == 0 and b == 0:
                    dve.wait_ge(gates_in, 16)
                dve.wait_ge(rden_d, b + 1)
                dve.wait_ge(pv_pe, 2 * b + h + 1)
                if b > 0:
                    dve.wait_ge(x2_p, 2 * b)
                for n in range(HALF):
                    i = HALF * h + n
                    dve.scalar_tensor_tensor(y[:, i, :], C[1 - h][:, n * D:(n + 1) * D], rden[:, i:i + 1],
                                             gates[:, b, 0, :], ALU.mult, ALU.mult).then_inc(y_d, 1)

            def accumulate(b, j):
                n = NJ * b + j
                dve.wait_ge(relu_a, n + 1)
                dve.wait_ge(acc_d, n)
                dve.scalar_tensor_tensor(acc[b % 2][:, :], relu[j][:, :], w2c[:, j:j + 1], acc[b % 2][:, :],
                                         ALU.mult, ALU.add).then_inc(acc_d, 1)

            statistics(0, 0)

            dve.wait_ge(cT_pe, 1)
            dve.tensor_copy(cT[:, :], E[0][:, 0:KD * B]).then_inc(cT_sb, 1)
            dve.wait_ge(c_exped, 1)
            dve.tensor_scalar(cT_den[:, :], cT_exp[:, :], 1.0, None, ALU.add).then_inc(c_steps, 1)
            dve.wait_ge(c_steps, 1)
            dve.reciprocal(cT_sig[:, :], cT_den[:, :]).then_inc(c_steps, 1)
            dve.wait_ge(c_steps, 2)
            dve.tensor_tensor(siluT[:, :, :].rearrange("p k b -> p (k b)"), cT[:, :], cT_sig[:, :],
                              ALU.mult).then_inc(siluT_sb, 1)

            def mod_columns(n, slot):
                dve.wait_ge(mod_pe, n + 1)
                for q in range(2):
                    o = (2 * n + q) * KD * B
                    ins = dve.tensor_scalar(mod[:, 2 * slot + q, :, :],
                                            E[1][:, o:o + KD * B].rearrange("p (k b) -> p k b", k=KD),
                                            float(q), None, ALU.add)
                ins.then_inc(mod_sb, 1)

            mod_columns(0, 0)

            def low_m(k):
                dve.wait_ge(m_hi_sb, k + 1)
                dve.scalar_tensor_tensor(m_lo[:, k, :], C[k][:, 0:D], SCALE, f(m_hi[:, k, :]),
                                         ALU.mult, ALU.subtract).then_inc(m_lo_sb, 1)

            dve.wait_ge(wv_in, 16)
            dve.tensor_copy(wv_hi[:, :, :], wv[:, :, :]).then_inc(w_hi_sb, 1)
            dve.wait_ge(w_hi_sb, 1)
            dve.tensor_tensor(wv_lo[:, :, :], wv[:, :, :], f(wv_hi[:, :, :]), ALU.subtract).then_inc(w_lo_sb, 1)

            def set_up_gates():
                dve.wait_ge(mod_pe, 2)
                cols = E[1][:, 2 * KD * B:4 * KD * B]
                dve.tensor_scalar(gateT_sign[:, :], cols, 0.0, 2.0, ALU.is_ge, ALU.mult).then_inc(gate_steps, 1)
                dve.tensor_scalar(gateT_pos[:, :], cols, GATE_MIN, None, ALU.max).then_inc(gate_steps, 1)
                dve.tensor_scalar(gateT_neg[:, :], cols, -1.0, GATE_MIN, ALU.mult, ALU.max).then_inc(gate_steps, 1)
                dve.wait_ge(gate_steps, 3)
                dve.tensor_tensor(gateT_abs[:, :], gateT_pos[:, :], gateT_neg[:, :], ALU.max).then_inc(gate_steps, 1)
                dve.wait_ge(gate_steps, 4)
                dve.scalar_tensor_tensor(gateT[:, :], gateT_sign[:, :], -1.0, gateT_abs[:, :], ALU.add,
                                         ALU.mult).then_inc(gate_steps, 1)

            def copy_gate_rows():
                dve.wait_ge(gate_pe, 1)
                dve.tensor_copy(gate[:, :, :], C[1][0:B, :].rearrange("b (n d) -> b n d", n=2)).then_inc(gate_rows, 1)

            def set_up_ffn():
                dve.wait_ge(bout_in, 16)
                dve.wait_ge(gate_rows, 1)
                dve.tensor_tensor(boutg[:, :], bout_sb[:, :], gate[:, 1, :], ALU.mult).then_inc(bout_steps, 1)
                dve.wait_ge(bout_steps, 1)
                dve.tensor_copy(boutg_hi[:, :], boutg[:, :]).then_inc(bout_steps, 1)
                dve.wait_ge(bout_steps, 2)
                dve.tensor_tensor(boutg_lo[:, :], boutg[:, :], f(boutg_hi[:, :]), ALU.subtract).then_inc(bout_steps, 1)
                dve.wait_ge(small_in, 11 * 16)
                dve.tensor_scalar(relu_bias[:, :], w1c[:, :], binc[:, 0:1], None, ALU.mult).then_inc(rbias, 1)
                dve.wait_ge(rbias, 1)
                dve.tensor_tensor(relu_bias[:, :], relu_bias[:, :], b1c[:, :], ALU.add).then_inc(rbias, 1)

            def step(i, live):
                if live(i - 1):
                    row_max(i - 1, 0)
                if i == 1:
                    copy_gate_rows()
                if live(i - 2):
                    weigh(i - 2, 1)
                if live(i - 3):
                    accumulate(i - 3, 4)
                if live(i - 1):
                    row_max(i - 1, 1)
                if live(i - 3):
                    accumulate(i - 3, 5)
                if live(i - 2):
                    token_stats(1, i - 2, 1)
                    aggregate(1, i - 2)
                if live(i - 1):
                    row_max(i - 1, 2)
                    low_v(i - 1, 0)
                    low_v(i - 1, 1)
                    row_max(i - 1, 3)
                    low_pt(i - 1, 0)
                if i == 1:
                    mod_columns(2, 1)
                if live(i - 1):
                    low_pt(i - 1, 1)
                if live(i - 3):
                    accumulate(i - 3, 6)
                if i == 0:
                    low_m(1)
                if live(i - 3):
                    accumulate(i - 3, 7)
                if live(i):
                    low_h(i, 1)
                if live(i - 1):
                    recip(i - 1)
                    low_pt(i - 1, 2)
                if live(i + 1) and i > 0:
                    token_stats(0, i + 1, 0)
                if i == 0:
                    statistics(0, 1)
                if live(i + 1) and i > 0:
                    token_stats(0, i + 1, 1)
                if live(i - 1):
                    weigh(i - 1, 0)
                if live(i):
                    low_t(i, 0)
                if i == 0:
                    set_up_gates()
                if live(i + 1) and i > 0:
                    aggregate(0, i + 1)
                if live(i - 2):
                    accumulate(i - 2, 1)
                if live(i):
                    low_t(i, 1)
                if live(i - 2):
                    accumulate(i - 2, 2)
                if live(i - 1):
                    token_stats(1, i - 1, 0)
                if live(i - 2):
                    accumulate(i - 2, 3)

            def run(i, live):
                if i == 2:
                    set_up_ffn()
                if i >= 0:
                    step(i, live)

            low_m(0)
            steps(run)

            def end_aggregate(h):
                dve.wait_ge(x2_p, 2 * (B - 1) + h + 1)
                if h == 0:
                    dve.wait_ge(aggr_d[1], NT * (B - 1))
                q = slice(HALF * h, HALF * (h + 1))
                for i in range(HALF * h, HALF * (h + 1)):
                    dve.bn_stats(stat[1][:, i, :], xs[:, B - 1, i, :]).then_inc(end_stat, 1)
                if h == 0:
                    dve.wait_ge(veps_d[1], B - 1)
                    dve.wait_ge(negmean_d[1], B - 1)
                for i in range(HALF * h, HALF * (h + 1)):
                    dve.wait_ge(end_stat, i + 1)
                    dve.bn_aggr(mv[1][:, i, :], stat[1][:, i, :]).then_inc(end_aggr, 1)
                dve.wait_ge(end_aggr, HALF * (h + 1))
                if h == 0:
                    dve.wait_ge(xn_p[1], NT * (B - 1))
                dve.tensor_scalar(veps[1][:, q], mv[1][:, q, 1], EPS, None, ALU.add).then_inc(end_var, 1)
                dve.tensor_scalar(negmean[1][:, q], mv[1][:, q, 0], -1.0, None, ALU.mult).then_inc(end_var, 1)

            def end_accumulate(h, j):
                q = slice(HALF * P * h, HALF * P * (h + 1))
                a = acc[(B - 1) % 2][:, q]
                dve.wait_ge(end_relu, NJ * h + j + 1)
                dve.wait_ge(end_acc[h], j)
                dve.scalar_tensor_tensor(a, relu[j][:, q], w2c[:, j:j + 1], a, ALU.mult, ALU.add).then_inc(end_acc[h], 1)

            def end_finish(i):
                h, n = i // HALF, i % HALF
                dve.wait_ge(end_o, i + 1)
                dve.tensor_tensor(xs[:, B - 1, i, :], (E, C)[h][n][:, 0:D], xs[:, B - 1, i, :],
                                  ALU.add).then_inc(end_fin, 1)

            row_max(B - 1, 0)
            weigh(B - 2, 1)
            row_max(B - 1, 1)
            accumulate(B - 3, 4)
            token_stats(1, B - 2, 1)
            aggregate(1, B - 2)
            row_max(B - 1, 2)
            low_v(B - 1, 0)
            low_v(B - 1, 1)
            row_max(B - 1, 3)
            low_pt(B - 1, 0)
            for j in range(5, 7):
                accumulate(B - 3, j)
            low_pt(B - 1, 1)
            accumulate(B - 3, 7)
            recip(B - 1)
            weigh(B - 1, 0)
            low_pt(B - 1, 2)
            end_aggregate(0)
            accumulate(B - 2, 1)
            weigh(B - 1, 1)
            for j in range(2, 4):
                accumulate(B - 2, j)
            end_aggregate(1)
            for j in range(4, 7):
                accumulate(B - 2, j)
            end_accumulate(0, 1)
            accumulate(B - 2, 7)
            for j in range(2, NJ):
                end_accumulate(0, j)
            for j in range(1, NJ):
                end_accumulate(1, j)
            end_finish(0)
            end_finish(1)
            end_finish(2)
            end_finish(3)


_IN = ["L0_attn_x", "L0_attn_WQ", "L0_attn_WK", "L0_attn_WV", "L0_ffn_Win", "L0_ffn_bin_", "L0_ffn_W1",
       "L0_ffn_b1", "L0_ffn_W2", "L0_ffn_b2", "L0_ffn_Wout", "L0_ffn_bout", "L0_c", "L0_wmod"]


def kernel(**inputs):
    import numpy as np
    import concourse.bacc as bacc
    from concourse.bass_utils import run_bass_kernel_spmd

    nc = bacc.Bacc("TRN2", target_bir_lowering=False, num_devices=1)
    arrays, args = {}, []
    for name in _IN:
        a = np.ascontiguousarray(inputs[name])
        arrays[name] = a
        args.append(nc.dram_tensor(name, a.shape, mybir.dt.from_np(a.dtype), kind="ExternalInput").ap())
    out = nc.dram_tensor("out", arrays["L0_attn_x"].shape, mybir.dt.float32, kind="ExternalOutput").ap()
    adaln_layer(nc, *args, out)
    return run_bass_kernel_spmd(nc, [arrays], core_ids=[0]).results[0]["out"]
```
